# Optimizing a Trainium2 kernel written in Bass

```python
import numpy as np
import jax
import jax.numpy as jnp

def _softmax(x, axis=-1):
    return jax.nn.softmax(x, axis=axis)

def _gelu(x):
    return jax.nn.gelu(x, approximate=True)

def _silu(x):
    return jax.nn.silu(x)

def _sigmoid(x):
    return jax.nn.sigmoid(x)

def _layernorm(x, axis=-1, eps=1e-05):
    m = jnp.mean(x, axis=axis, keepdims=True)
    v = jnp.var(x, axis=axis, keepdims=True)
    return (x - m) / jnp.sqrt(v + eps)

def _scatter_add(tgt, idx, src, axis=0):
    return tgt.at[idx].add(src)

def _segment_sum(src, seg, n):
    return jax.ops.segment_sum(src, seg, n)
kernel_name = 'mk_decoder_postln_d1_seqx_r8_f59990'

def setup_inputs(seed: int=0):
    np.random.seed(seed)
    _w = jnp.asarray

    def _rec_inputs():
        import jax
        import jax.numpy as jnp
        _rk = jax.random.key(seed)
        x = -0.0005207 + 1.001 * jax.random.normal(jax.random.fold_in(_rk, 1), (4, 256, 128), jnp.float32)
        _lenS = 256 - jax.random.randint(jax.random.fold_in(_rk, 7), (4,), 0, max(1, 256 // 4) + 1, jnp.int32)
        _lenS2 = 512 - jax.random.randint(jax.random.fold_in(_rk, 8), (4,), 0, max(1, 512 // 4) + 1, jnp.int32)
        _ctx_1024P = jax.random.normal(jax.random.fold_in(_rk, 11), (4, 16, 128), jnp.float32)
        _ctx_1024c = jax.random.dirichlet(jax.random.fold_in(_rk, 511), 0.3 * jnp.ones((16,), jnp.float32), (4, 512))
        _ctx_1024t = jnp.einsum('bsk,bkd->bsd', _ctx_1024c, _ctx_1024P)
        _ctx_1024t = _ctx_1024t * jax.lax.rsqrt(jnp.mean(jnp.square(_ctx_1024t)) + 1e-12) * 0.953939
        ctx_1024 = -1.52775e-05 + 0.999936 * (_ctx_1024t + 0.3 * jax.random.normal(jax.random.fold_in(_rk, 611), (4, 512, 128), jnp.float32))
        return (x, ctx_1024)
    x, ctx_1024 = _rec_inputs()

    def _L0_attn_setup():
        import jax, jax.numpy as jnp
        import numpy as np
        INFTY_APPROX = 1e+30
        ROTARY_BASE = 10000.0
        D_HEAD = 128

        def rope(x, base=ROTARY_BASE):
            *_, length, width = x.shape
            half = width // 2
            positions = jnp.arange(length)[:, None].astype(jnp.float32)
            ang_freqs = jnp.power(base, -jnp.arange(half) / half)[None, :]
            radians = positions * ang_freqs
            cos = jnp.cos(radians).astype(x.dtype)[None, None]
            sin = jnp.sin(radians).astype(x.dtype)[None, None]
            even, odd = jnp.split(x, 2, axis=-1)
            return jnp.concatenate([even * cos - odd * sin, even * sin + odd * cos], axis=-1)
        key = jax.random.key(seed)
        ks = jax.random.split(key, 5)
        B, T, M, H, D = (2, 256, 128, 8, D_HEAD)
        x = jax.random.normal(ks[0], (B, T, M), dtype=jnp.float32)
        scale = M ** (-0.5)
        wq = jax.random.normal(ks[1], (M, H, D), dtype=jnp.float32) * scale
        wk = jax.random.normal(ks[2], (M, H, D), dtype=jnp.float32) * scale
        wv = jax.random.normal(ks[3], (M, H, D), dtype=jnp.float32) * scale
        wo = jax.random.normal(ks[4], (H, D, M), dtype=jnp.float32) * scale
        return {'x': x, 'wq': wq, 'wk': wk, 'wv': wv, 'wo': wo}
    _L0_attn_all = _L0_attn_setup()
    _L0_attn_in = {k: v for k, v in _L0_attn_all.items() if k in ('wq', 'wk', 'wv', 'wo')}
    del _L0_attn_all

    def _L0_xattn_setup():
        import jax, jax.numpy as jnp
        import numpy as np
        DIM = 128
        HEADS = 16
        DHEAD = 64
        INNER = HEADS * DHEAD
        EPS = 1e-05

        def layer_norm(x, g, b):
            mu = jnp.mean(x, axis=-1, keepdims=True)
            var = jnp.mean(jnp.square(x - mu), axis=-1, keepdims=True)
            return (x - mu) * jax.lax.rsqrt(var + EPS) * g + b

        def apply_rope(x, cos, sin):
            d2 = x.shape[-1] // 2
            x1, x2 = (x[..., :d2], x[..., d2:])
            return jnp.concatenate([x1 * cos - x2 * sin, x2 * cos + x1 * sin], axis=-1)
        key = jax.random.key(seed)
        ks = jax.random.split(key, 10)
        B, N, S = (8, 32, 512)
        latents = jax.random.normal(ks[0], (B, N, DIM), dtype=jnp.float32)
        context = jax.random.normal(ks[1], (B, S, DIM), dtype=jnp.float32)
        cos = jax.random.uniform(ks[2], (S, DHEAD // 2), dtype=jnp.float32)
        sin = jax.random.uniform(ks[3], (S, DHEAD // 2), dtype=jnp.float32)
        init = lambda k, shp, fan_in: jax.random.normal(k, shp, dtype=jnp.float32) / np.sqrt(fan_in)
        return {'latents': latents, 'context': context, 'cos': cos, 'sin': sin, 'ln_lat_g': jnp.ones((DIM,), jnp.float32), 'ln_lat_b': jnp.zeros((DIM,), jnp.float32), 'ln_ctx_g': jnp.ones((DIM,), jnp.float32), 'ln_ctx_b': jnp.zeros((DIM,), jnp.float32), 'Wq': init(ks[4], (DIM, INNER), DIM), 'Wkv': init(ks[5], (DIM, 2 * INNER), DIM), 'Wo': init(ks[6], (INNER, DIM), INNER), 'bo': jnp.zeros((DIM,), jnp.float32)}
    _L0_xattn_all = _L0_xattn_setup()
    _L0_xattn_in = {k: v for k, v in _L0_xattn_all.items() if k in ('cos', 'sin', 'ln_lat_g', 'ln_lat_b', 'ln_ctx_g', 'ln_ctx_b', 'Wq', 'Wkv', 'Wo', 'bo')}
    del _L0_xattn_all

    def _L0_ffn_setup():
        import jax, jax.numpy as jnp
        import numpy as np
        D_MODEL = 128
        N_HEADS = 16
        HEAD_DIM = D_MODEL // N_HEADS
        FFN_DIM = 512
        N_EXPERTS = 8
        TOP_K = 2
        BATCH = 4
        SEQ = 128

        def _layernorm(x, w, b, eps=1e-05):
            mu = jnp.mean(x, axis=-1, keepdims=True)
            var = jnp.mean(jnp.square(x - mu), axis=-1, keepdims=True)
            return (x - mu) * jax.lax.rsqrt(var + eps) * w + b

        def _causal_attention(nx, Wqkv, bqkv, Wo, bo):
            B, S, D = nx.shape
            qkv = nx @ Wqkv + bqkv
            q, k, v = jnp.split(qkv, 3, axis=-1)
            q = q.reshape(B, S, N_HEADS, HEAD_DIM)
            k = k.reshape(B, S, N_HEADS, HEAD_DIM)
            v = v.reshape(B, S, N_HEADS, HEAD_DIM)
            scores = jnp.einsum('bqhd,bkhd->bhqk', q, k) / jnp.sqrt(jnp.float32(HEAD_DIM))
            causal = jnp.tril(jnp.ones((S, S), bool))
            scores = jnp.where(causal, scores, jnp.finfo(scores.dtype).min)
            attn = jax.nn.softmax(scores, axis=-1)
            out = jnp.einsum('bhqk,bkhd->bqhd', attn, v).reshape(B, S, D)
            return out @ Wo + bo

        def _moe_ffn(nx, gate_W, fc1_w, fc1_b, fc2_w, fc2_b):
            gate_logits = nx @ gate_W
            topk_vals, topk_idx = jax.lax.top_k(gate_logits, TOP_K)
            gate_w = jax.nn.softmax(topk_vals, axis=-1)
            dense_gates = jnp.sum(jax.nn.one_hot(topk_idx, N_EXPERTS, dtype=nx.dtype) * gate_w[..., None], axis=-2)
            moe_out = jnp.zeros_like(nx)
            for e in range(N_EXPERTS):
                h = jax.nn.gelu(jnp.einsum('bsd,fd->bsf', nx, fc1_w[e]) + fc1_b[e], approximate=False)
                y = jnp.einsum('bsf,df->bsd', h, fc2_w[e]) + fc2_b[e]
                moe_out = moe_out + y * dense_gates[..., e:e + 1]
            return moe_out
        key = jax.random.key(seed)
        ks = jax.random.split(key, 12)
        s = lambda k, shape, scale: jax.random.normal(k, shape, dtype=jnp.float32) * scale
        inp = {'x': s(ks[0], (BATCH, SEQ, D_MODEL), 1.0), 'ln1_w': jnp.ones((D_MODEL,), jnp.float32), 'ln1_b': jnp.zeros((D_MODEL,), jnp.float32), 'ln2_w': jnp.ones((D_MODEL,), jnp.float32), 'ln2_b': jnp.zeros((D_MODEL,), jnp.float32), 'Wqkv': s(ks[1], (D_MODEL, 3 * D_MODEL), 0.02), 'bqkv': jnp.zeros((3 * D_MODEL,), jnp.float32), 'Wo': s(ks[2], (D_MODEL, D_MODEL), 0.02), 'bo': jnp.zeros((D_MODEL,), jnp.float32), 'gate_W': s(ks[3], (D_MODEL, N_EXPERTS), 0.02), 'fc1_w': s(ks[4], (N_EXPERTS, FFN_DIM, D_MODEL), (2.0 / D_MODEL) ** 0.5), 'fc1_b': jnp.zeros((N_EXPERTS, FFN_DIM), jnp.float32), 'fc2_w': s(ks[5], (N_EXPERTS, D_MODEL, FFN_DIM), (1.0 / FFN_DIM) ** 0.5), 'fc2_b': jnp.zeros((N_EXPERTS, D_MODEL), jnp.float32)}
        return inp
    _L0_ffn_all = _L0_ffn_setup()
    _L0_ffn_in = {k: v for k, v in _L0_ffn_all.items() if k in ('ln1_w', 'ln1_b', 'ln2_w', 'ln2_b', 'Wqkv', 'bqkv', 'Wo', 'bo', 'gate_W', 'fc1_w', 'fc1_b', 'fc2_w', 'fc2_b')}
    del _L0_ffn_all
    return {'x': x, 'ctx_1024': ctx_1024, 'L0_attn_wq': _L0_attn_in['wq'], 'L0_attn_wk': _L0_attn_in['wk'], 'L0_attn_wv': _L0_attn_in['wv'], 'L0_attn_wo': _L0_attn_in['wo'], 'L0_xattn_cos': _L0_xattn_in['cos'], 'L0_xattn_sin': _L0_xattn_in['sin'], 'L0_xattn_ln_lat_g': _L0_xattn_in['ln_lat_g'], 'L0_xattn_ln_lat_b': _L0_xattn_in['ln_lat_b'], 'L0_xattn_ln_ctx_g': _L0_xattn_in['ln_ctx_g'], 'L0_xattn_ln_ctx_b': _L0_xattn_in['ln_ctx_b'], 'L0_xattn_Wq': _L0_xattn_in['Wq'], 'L0_xattn_Wkv': _L0_xattn_in['Wkv'], 'L0_xattn_Wo': _L0_xattn_in['Wo'], 'L0_xattn_bo': _L0_xattn_in['bo'], 'L0_ffn_ln1_w': _L0_ffn_in['ln1_w'], 'L0_ffn_ln1_b': _L0_ffn_in['ln1_b'], 'L0_ffn_ln2_w': _L0_ffn_in['ln2_w'], 'L0_ffn_ln2_b': _L0_ffn_in['ln2_b'], 'L0_ffn_Wqkv': _L0_ffn_in['Wqkv'], 'L0_ffn_bqkv': _L0_ffn_in['bqkv'], 'L0_ffn_Wo': _L0_ffn_in['Wo'], 'L0_ffn_bo': _L0_ffn_in['bo'], 'L0_ffn_gate_W': _L0_ffn_in['gate_W'], 'L0_ffn_fc1_w': _L0_ffn_in['fc1_w'], 'L0_ffn_fc1_b': _L0_ffn_in['fc1_b'], 'L0_ffn_fc2_w': _L0_ffn_in['fc2_w'], 'L0_ffn_fc2_b': _L0_ffn_in['fc2_b']}

def reference(x, ctx_1024, L0_attn_wq, L0_attn_wk, L0_attn_wv, L0_attn_wo, L0_xattn_cos, L0_xattn_sin, L0_xattn_ln_lat_g, L0_xattn_ln_lat_b, L0_xattn_ln_ctx_g, L0_xattn_ln_ctx_b, L0_xattn_Wq, L0_xattn_Wkv, L0_xattn_Wo, L0_xattn_bo, L0_ffn_ln1_w, L0_ffn_ln1_b, L0_ffn_ln2_w, L0_ffn_ln2_b, L0_ffn_Wqkv, L0_ffn_bqkv, L0_ffn_Wo, L0_ffn_bo, L0_ffn_gate_W, L0_ffn_fc1_w, L0_ffn_fc1_b, L0_ffn_fc2_w, L0_ffn_fc2_b):
    import jax
    import jax.numpy as jnp

    def _L0_attn_ref(x, wq, wk, wv, wo):
        import jax, jax.numpy as jnp
        import numpy as np
        INFTY_APPROX = 1e+30
        ROTARY_BASE = 10000.0
        D_HEAD = 128

        def rope(x, base=ROTARY_BASE):
            *_, length, width = x.shape
            half = width // 2
            positions = jnp.arange(length)[:, None].astype(jnp.float32)
            ang_freqs = jnp.power(base, -jnp.arange(half) / half)[None, :]
            radians = positions * ang_freqs
            cos = jnp.cos(radians).astype(x.dtype)[None, None]
            sin = jnp.sin(radians).astype(x.dtype)[None, None]
            even, odd = jnp.split(x, 2, axis=-1)
            return jnp.concatenate([even * cos - odd * sin, even * sin + odd * cos], axis=-1)
        B, T, M = x.shape
        q = jnp.einsum('bim,mhd->bhid', x, wq)
        k = jnp.einsum('bim,mhd->bhid', x, wk)
        v = jnp.einsum('bim,mhd->bhid', x, wv)
        q = rope(q)
        k = rope(k)
        s = jnp.einsum('bhid,bhjd->bhij', q, k) / jnp.asarray(D_HEAD, q.dtype)
        i = jnp.arange(T)[:, None]
        j = jnp.arange(T)[None, :]
        mask = (i < j)[None, None]
        s = s - jnp.asarray(INFTY_APPROX, s.dtype) * mask
        p = jax.nn.softmax(s, axis=-1)
        o = jnp.einsum('bhij,bhjd->bhid', p, v)
        return jnp.einsum('bhid,hdm->bim', o, wo)

    def _L0_xattn_ref(latents, context, cos, sin, ln_lat_g, ln_lat_b, ln_ctx_g, ln_ctx_b, Wq, Wkv, Wo, bo):
        import jax, jax.numpy as jnp
        import numpy as np
        DIM = 128
        HEADS = 16
        DHEAD = 64
        INNER = HEADS * DHEAD
        EPS = 1e-05

        def layer_norm(x, g, b):
            mu = jnp.mean(x, axis=-1, keepdims=True)
            var = jnp.mean(jnp.square(x - mu), axis=-1, keepdims=True)
            return (x - mu) * jax.lax.rsqrt(var + EPS) * g + b

        def apply_rope(x, cos, sin):
            d2 = x.shape[-1] // 2
            x1, x2 = (x[..., :d2], x[..., d2:])
            return jnp.concatenate([x1 * cos - x2 * sin, x2 * cos + x1 * sin], axis=-1)
        b, n, _ = latents.shape
        s = context.shape[1]
        lat = layer_norm(latents, ln_lat_g, ln_lat_b)
        ctx = layer_norm(context, ln_ctx_g, ln_ctx_b)
        q = (lat @ Wq).reshape(b, n, HEADS, DHEAD).transpose(0, 2, 1, 3)
        kv = ctx @ Wkv
        k, v = jnp.split(kv, 2, axis=-1)
        k = k.reshape(b, s, HEADS, DHEAD).transpose(0, 2, 1, 3)
        v = v.reshape(b, s, HEADS, DHEAD).transpose(0, 2, 1, 3)
        k = apply_rope(k, cos[None, None], sin[None, None])
        scale = DHEAD ** (-0.5)
        attn = jnp.einsum('bhnd,bhsd->bhns', q, k) * scale
        attn = jnp.clip(attn, -11.0, 11.0)
        attn = jax.nn.softmax(attn, axis=-1)
        out = jnp.einsum('bhns,bhsd->bhnd', attn, v)
        out = out.transpose(0, 2, 1, 3).reshape(b, n, INNER)
        return out @ Wo + bo

    def _L0_ffn_ref(x, ln1_w, ln1_b, ln2_w, ln2_b, Wqkv, bqkv, Wo, bo, gate_W, fc1_w, fc1_b, fc2_w, fc2_b):
        import jax, jax.numpy as jnp
        import numpy as np
        D_MODEL = 128
        N_HEADS = 16
        HEAD_DIM = D_MODEL // N_HEADS
        FFN_DIM = 512
        N_EXPERTS = 8
        TOP_K = 2
        BATCH = 4
        SEQ = 128

        def _layernorm(x, w, b, eps=1e-05):
            mu = jnp.mean(x, axis=-1, keepdims=True)
            var = jnp.mean(jnp.square(x - mu), axis=-1, keepdims=True)
            return (x - mu) * jax.lax.rsqrt(var + eps) * w + b

        def _causal_attention(nx, Wqkv, bqkv, Wo, bo):
            B, S, D = nx.shape
            qkv = nx @ Wqkv + bqkv
            q, k, v = jnp.split(qkv, 3, axis=-1)
            q = q.reshape(B, S, N_HEADS, HEAD_DIM)
            k = k.reshape(B, S, N_HEADS, HEAD_DIM)
            v = v.reshape(B, S, N_HEADS, HEAD_DIM)
            scores = jnp.einsum('bqhd,bkhd->bhqk', q, k) / jnp.sqrt(jnp.float32(HEAD_DIM))
            causal = jnp.tril(jnp.ones((S, S), bool))
            scores = jnp.where(causal, scores, jnp.finfo(scores.dtype).min)
            attn = jax.nn.softmax(scores, axis=-1)
            out = jnp.einsum('bhqk,bkhd->bqhd', attn, v).reshape(B, S, D)
            return out @ Wo + bo

        def _moe_ffn(nx, gate_W, fc1_w, fc1_b, fc2_w, fc2_b):
            gate_logits = nx @ gate_W
            topk_vals, topk_idx = jax.lax.top_k(gate_logits, TOP_K)
            gate_w = jax.nn.softmax(topk_vals, axis=-1)
            dense_gates = jnp.sum(jax.nn.one_hot(topk_idx, N_EXPERTS, dtype=nx.dtype) * gate_w[..., None], axis=-2)
            moe_out = jnp.zeros_like(nx)
            for e in range(N_EXPERTS):
                h = jax.nn.gelu(jnp.einsum('bsd,fd->bsf', nx, fc1_w[e]) + fc1_b[e], approximate=False)
                y = jnp.einsum('bsf,df->bsd', h, fc2_w[e]) + fc2_b[e]
                moe_out = moe_out + y * dense_gates[..., e:e + 1]
            return moe_out
        nx = _layernorm(x, ln1_w, ln1_b)
        attn_out = _causal_attention(nx, Wqkv, bqkv, Wo, bo)
        x = x + attn_out
        nx2 = _layernorm(x, ln2_w, ln2_b)
        moe_out = _moe_ffn(nx2, gate_W, fc1_w, fc1_b, fc2_w, fc2_b)
        return x + moe_out
    x = _layernorm(x + _L0_attn_ref(x, L0_attn_wq, L0_attn_wk, L0_attn_wv, L0_attn_wo), axis=-1)
    x = _layernorm(x + _L0_xattn_ref(x, ctx_1024, L0_xattn_cos, L0_xattn_sin, L0_xattn_ln_lat_g, L0_xattn_ln_lat_b, L0_xattn_ln_ctx_g, L0_xattn_ln_ctx_b, L0_xattn_Wq, L0_xattn_Wkv, L0_xattn_Wo, L0_xattn_bo), axis=-1)
    x = _layernorm(x + _L0_ffn_ref(x, L0_ffn_ln1_w, L0_ffn_ln1_b, L0_ffn_ln2_w, L0_ffn_ln2_b, L0_ffn_Wqkv, L0_ffn_bqkv, L0_ffn_Wo, L0_ffn_bo, L0_ffn_gate_W, L0_ffn_fc1_w, L0_ffn_fc1_b, L0_ffn_fc2_w, L0_ffn_fc2_b), axis=-1)
    return x

_drawn_inputs = setup_inputs


def setup_inputs(seed=0):
    import zlib

    import numpy as np

    out = dict(_drawn_inputs(seed))
    spreads = {'L0_xattn_ln_lat_g': (1.0, 0.2),
     'L0_xattn_ln_lat_b': (0.0, 0.1),
     'L0_xattn_ln_ctx_g': (1.0, 0.2),
     'L0_xattn_ln_ctx_b': (0.0, 0.1),
     'L0_xattn_bo': (0.0, 0.1),
     'L0_ffn_ln1_w': (1.0, 0.2),
     'L0_ffn_ln1_b': (0.0, 0.303),
     'L0_ffn_ln2_w': (1.0, 0.2),
     'L0_ffn_ln2_b': (0.0, 0.1),
     'L0_ffn_bqkv': (0.0, 0.1),
     'L0_ffn_bo': (0.0, 0.1),
     'L0_ffn_fc1_b': (0.0, 0.346),
     'L0_ffn_fc2_b': (0.0, 0.1)}
    factors = {}
    for name, (base, spread) in spreads.items():
        noise = np.random.default_rng([zlib.crc32(name.encode()), seed]).standard_normal(out[name].shape)
        drawn = base * np.exp(spread * noise) if base else spread * noise
        out[name] = jnp.asarray(drawn.astype(out[name].dtype))
    for name, factor in factors.items():
        out[name] = (out[name] * factor).astype(out[name].dtype)
    return out
```

```python
from contextlib import ExitStack

import numpy as np

import concourse.bass as bass
from concourse import mybir

F32 = mybir.dt.float32
F32R = mybir.dt.float32r
BF16 = mybir.dt.bfloat16
U32 = mybir.dt.uint32
ALU = mybir.AluOpType
ACT = mybir.ActivationFunctionType
AX = mybir.AxisListType

P = 128
D = 128
B, S = 4, 256
T = B * S
NT = T // P
SC = 512
CT = B * SC // P
AH = 8
XH, XD = 16, 64
HP = XH // 2
FH, FD = 16, 8
NQ = FH // 4
E, FF = 8, 512
FT = FF // P
EPS = 1e-5
MASKED = -1e30
CLIP_LO, CLIP_HI = float(np.exp(np.float32(-11.0))), float(np.exp(np.float32(11.0)))

C_ID, C_MASK, C_IOTA, C_AB, C_SEL = 0, P, 2 * P, 2 * P + 8, 2 * P + 12
N_CONST = C_SEL + E * P
V_CTX, V_LAT, V_LN1, V_LN2, V_BQK = 0, 2, 4, 6, 8
N_VEC = V_BQK + 2 * NQ
W1, W2, WB = 0, FF, 2 * FF
N_EXP = 2 * FF + FT


def wait(eng, sem, n):
    if not isinstance(n, int) or n > 0:
        eng.wait_ge(sem, n)


def at(h, c, skew):
    h, c = h + (c - skew) // 4, (c - skew) % 4
    return h, c, 4 * h + c


def live(u, n):
    return not isinstance(u, int) or 0 <= u < n


def capped(n, most):
    return min(n, most) if isinstance(n, int) else n


def pipeline(eng, groups, step, skew):
    for k in range(8):
        step(k // 4, k % 4)
    with eng.Fori(2, groups) as h:
        for c in range(4):
            step(h, c)
    for k in range(4 * groups, 4 * groups + skew):
        step(k // 4, k % 4)


def build_program(nc, a, out):
    with ExitStack() as ctx:
        build(nc, ctx, a, out)


def build(nc, ctx, a, out):
    def sb(name, shape, dt=F32, stack=ctx):
        return stack.enter_context(nc.sbuf_tensor(name, shape, dt))

    def sem(name):
        return ctx.enter_context(nc.semaphore(name))

    PS = ctx.enter_context(nc.psum_tensor("PS", [P, 8, 512], F32))

    def bank(i):
        return PS[:, i, :]

    const = sb("const", [P, N_CONST])
    ident = const[:, C_ID:C_ID + P]
    ident16 = sb("ident16", [P, P], BF16)
    mask16 = sb("mask16", [P, 3, P], BF16)
    vec = sb("vec", [P, N_VEC])
    rows = sb("rows", [P, 3, D])
    x_tok = sb("x_tok", [P, NT, D])
    resid = sb("resid", [P, NT, D])
    x1 = sb("x1", [P, NT, D])
    x2 = sb("x2", [P, NT, D])
    norm = sb("norm", [P, CT, D])
    featT = sb("featT", [P, CT * P])
    stats = sb("stats", [P, CT, 6])
    mv = sb("mv", [P, CT, 2])
    rstd = sb("rstd", [P, CT])
    half = sb("half", [P, CT])
    OT = sb("OT", [P, 8, T])
    wo = sb("wo", [P, 8, D])
    f_wqk = sb("f_wqk", [P, 2 * NQ * P])
    f_wvo = sb("f_wvo", [P, 2, D])
    gate_w = sb("gate_w", [P, E])
    fc2_b = sb("fc2_b", [2 * E, D])

    in_const, in_x, in_aw, in_ctx, in_xw, in_fw, in_ex = (sem(n) for n in (
        "in_const", "in_x", "in_aw", "in_ctx", "in_xw", "in_fw", "in_ex"))
    ln_raw, ln_stats, ln_eps, ln_rstd, ln_out = (sem(n) for n in (
        "ln_raw", "ln_stats", "ln_eps", "ln_rstd", "ln_out"))
    nt_pe, nt_act, nt_hi, nt_lo = (sem(n) for n in ("nt_pe", "nt_act", "nt_hi", "nt_lo"))

    def ln_vector(dve, n_ln, src, dst, n):
        for t in range(n):
            dve.bn_stats(stats[:, t, :], src[:, t, :]).then_inc(ln_raw, 1)
        for t in range(n):
            dve.wait_ge(ln_raw, n_ln + t + 1)
            dve.bn_aggr(mv[:, t, :], stats[:, t, :]).then_inc(ln_stats, 1)
        dve.wait_ge(ln_rstd, n_ln + n)
        for t in range(n):
            dve.tensor_scalar(dst[:, t, :], src[:, t, :], mv[:, t, 0:1], rstd[:, t:t + 1],
                              ALU.subtract, ALU.mult).then_inc(ln_out, 1)

    def ln_gpsimd(pool, n_ln, n):
        pool.wait_ge(ln_stats, n_ln + n)
        pool.tensor_scalar(rstd[:, 0:n], mv[:, 0:n, 1], EPS, None, ALU.add).then_inc(ln_eps, n)
        pool.wait_ge(ln_eps, n_ln + n)
        pool.tensor_tensor(rstd[:, 0:n], rstd[:, 0:n], half[:, 0:n], ALU.pow).then_inc(ln_rstd, n)

    def nt_tensor(pe, n_ln, n_nt, src, n, first_bank):
        for t in range(n):
            pe.wait_ge(ln_out, n_ln + t + 1)
            pe.transpose(PS[:, first_bank + t // 4, (t % 4) * P:(t % 4 + 1) * P],
                         src[:, t, :], ident).then_inc(nt_pe, 1)

    def nt_scalar(act, n_nt, n, first_bank, v):
        for j in range(n // 4):
            act.wait_ge(nt_pe, n_nt + 4 * j + 4)
            act.activation(featT[:, j * 512:(j + 1) * 512], bank(first_bank + j), ACT.Identity,
                           bias=vec[:, v + 1:v + 2], scale=vec[:, v:v + 1]).then_inc(nt_act, 4)

    def nt_split(dve, n_nt, n, hi, lo):
        for j in range(n // 4):
            c = slice(j * 512, (j + 1) * 512)
            dve.wait_ge(nt_act, n_nt + 4 * j + 4)
            dve.tensor_copy(hi[:, c], featT[:, c]).then_inc(nt_hi, 4)
            dve.wait_ge(nt_hi, n_nt + 4 * j + 4)
            dve.tensor_tensor(lo[:, c], featT[:, c], hi[:, c].bitcast(F32),
                              ALU.subtract).then_inc(nt_lo, 4)

    def mm3(pe, o, w_hi, w_lo, m_hi, m_lo, start=True, stop=True, **kw):
        pe.matmul(o, w_hi, m_hi, start=start, stop=False, **kw)
        pe.matmul(o, w_hi, m_lo, start=False, stop=False, **kw)
        return pe.matmul(o, w_lo, m_hi, start=False, stop=stop, **kw)

    xT_hi = sb("xT_hi", [P, T], F32R)
    xT_lo = sb("xT_lo", [P, T], F32R)
    cross = ExitStack()
    xw_hi = sb("xw_hi", [P, HP, 512], F32R, cross)
    xw_lo = sb("xw_lo", [P, HP, 512], F32R, cross)
    x_rope = sb("x_rope", [P, 2, 512], F32, cross)
    cT_hi = sb("cT_hi", [P, CT * P], F32R, cross)
    cT_lo = sb("cT_lo", [P, CT * P], F32R, cross)

    with ExitStack() as stage:
        ctx_raw = OT[:, 0:2, :].rearrange("p a (t d) -> p (a t) d", d=D)
        xw_raw = OT[:, 2:6, :].rearrange("p a (h n) -> p (a h) n", n=512)
        xT_raw = OT[:, 6, :]
        aw_raw = sb("aw_raw", [P, AH, 3 * P], F32, stage)
        aw_hi = sb("aw_hi", [P, AH * 3 * P], F32R, stage)
        aw_lo = sb("aw_lo", [P, AH * 3 * P], F32R, stage)
        a_rope = sb("a_rope", [P, 2, 512], F32, stage)
        rot = sb("rot", [P, 2, 3, 512], F32, stage)
        qkT = sb("qkT", [P, 2, 512], F32, stage)
        v_sb = sb("v_sb", [P, 2, 2, P], F32, stage)
        nmax = sb("nmax", [P, 2, 2], F32, stage)
        den = sb("den", [P, 2, 2], F32, stage)
        rden = sb("rden", [P, 2, 2], F32, stage)
        prob = sb("prob", [P, 2, 3 * P], F32, stage)
        pT = sb("pT", [P, 2, 3 * P], F32, stage)

        p_const, p_xhi, p_awhi, p_awlo, p_xwhi, p_sin, p_xwlo = (sem(n) for n in (
            "p_const", "p_xhi", "p_awhi", "p_awlo", "p_xwhi", "p_sin", "p_xwlo"))

        with nc.Block() as block:
            @block.sync
            def _(sp):
                sp.dma_start(xT_raw, a["xT"]).then_inc(in_x, 16)
                sp.dma_start(x_tok[:], a["x_tok"]).then_inc(in_x, 16)
                sp.dma_start(ctx_raw, a["ctx_tok"]).then_inc(in_ctx, 16)
                sp.dma_start(xw_raw, a["x_w"]).then_inc(in_xw, 16)
                sp.dma_start(x_rope[:], a["x_rope"]).then_inc(in_xw, 16)
                sp.dma_start(rows[:], a["rows"]).then_inc(in_fw, 16)
                sp.dma_start(f_wvo[:], a["f_wvo"]).then_inc(in_fw, 16)
                sp.dma_start(gate_w[:], a["gate_w"]).then_inc(in_fw, 16)
                sp.dma_start(fc2_b[:], a["fc2_b"]).then_inc(in_fw, 16)
                sp.dma_start(wo[:], a["a_wo"]).then_inc(in_fw, 16)
                sp.dma_start(f_wqk[:], a["f_wqk"]).then_inc(in_fw, 16)

            @block.scalar
            def _(act):
                act.dma_start(const[:], a["const"]).then_inc(in_const, 16)
                act.dma_start(vec[:], a["vec"]).then_inc(in_const, 16)
                act.dma_start(aw_raw[:], a["a_w"]).then_inc(in_aw, 16)
                act.dma_start(a_rope[:], a["a_rope"]).then_inc(in_aw, 16)
                act.wait_ge(in_const, 32)
                act.copy(ident16[:], ident).then_inc(p_const, 1)
                for j in (0, 2):
                    act.copy(mask16[:, j, :], const[:, C_MASK:C_MASK + P]).then_inc(p_const, 1)
                nt_scalar(act, 0, CT, 0, V_CTX)

            @block.gpsimd
            def _(pool):
                pool.memset(half[:], -0.5).then_inc(p_const, 1)
                pool.memset(mask16[:, 1, :], 0.0).then_inc(p_const, 1)
                pool.wait_ge(p_const, 5)
                ln_gpsimd(pool, 0, CT)
                pool.wait_ge(p_xwhi, HP)
                for h in range(HP):
                    pool.tensor_tensor(xw_lo[:, h, :], xw_raw[:, h, :],
                                       xw_hi[:, h, :].bitcast(F32), ALU.subtract).then_inc(p_xwlo, 1)

            @block.vector
            def _(dve):
                dve.wait_ge(in_x, 32)
                dve.tensor_copy(xT_hi[:], xT_raw).then_inc(p_xhi, 1)
                dve.wait_ge(p_xhi, 1)
                dve.tensor_tensor(xT_lo[:], xT_raw, xT_hi[:].bitcast(F32), ALU.subtract)\
                   .then_inc(p_xhi, 1)
                dve.wait_ge(in_aw, 32)
                aw = aw_raw[:].rearrange("p h n -> p (h n)")
                dve.tensor_copy(aw_hi[:], aw).then_inc(p_awhi, 1)
                dve.wait_ge(p_awhi, 1)
                dve.tensor_tensor(aw_lo[:], aw, aw_hi[:].bitcast(F32), ALU.subtract)\
                   .then_inc(p_awlo, 1)
                dve.wait_ge(in_ctx, 16)
                ln_vector(dve, 0, ctx_raw, norm, CT)
                dve.wait_ge(in_xw, 32)
                for h in range(HP):
                    dve.tensor_copy(xw_hi[:, h, :], xw_raw[:, h, :]).then_inc(p_xwhi, 1)
                sin = x_rope[:, 1, :].rearrange("p (s a i) -> p s a i", s=4, a=2)[:, :, 0, :]
                dve.tensor_scalar(sin, sin, -1.0, None, ALU.mult).then_inc(p_sin, 1)
                nt_split(dve, 0, CT, cT_hi, cT_lo)

            @block.tensor
            def _(pe):
                pe.wait_ge(in_const, 32)
                nt_tensor(pe, 0, 0, norm, CT, 0)

        QK, TB, SB, PT, VB, OB = 0, 2, 3, 5, 6, 7
        N = 4 * AH
        a_qk, a_t1, a_t2, a_sum, a_T, a_qkT, a_S, a_max, a_exp, a_rden, a_prob = (sem(n) for n in (
            "a_qk", "a_t1", "a_t2", "a_sum", "a_T", "a_qkT", "a_S", "a_max", "a_exp", "a_rden",
            "a_prob"))
        a_V, a_vsb, a_PT, a_pT, a_O, a_OT = (sem(n) for n in (
            "a_V", "a_vsb", "a_PT", "a_pT", "a_O", "a_OT"))

        with nc.Block() as block:
            @block.tensor
            def _(pe):
                def step(h, c):
                    hh, b, u = at(h, c, 0)
                    if live(u, N):
                        wait(pe, a_t2, u - 1)
                        for it in range(2):
                            t = slice(b * S + it * P, b * S + it * P + P)
                            ws = bass.ds(hh * 384, 256)
                            last = mm3(pe, PS[:, QK + c % 2, it * 256:it * 256 + 256],
                                       xT_hi[:, t], xT_lo[:, t], aw_hi[:, ws], aw_lo[:, ws])
                        last.then_inc(a_qk, 1)
                    hh, b, u = at(h, c, 1)
                    if live(u, N):
                        wait(pe, a_sum, u + 1)
                        wait(pe, a_qkT, u)
                        for j in range(4):
                            src = rot[:, b % 2, 2, :].rearrange("p (t q d) -> p q t d", t=2, q=2)
                            last = pe.transpose(PS[:, TB, j * P:(j + 1) * P],
                                                src[:, j // 2, j % 2, :], ident)
                        last.then_inc(a_T, 1)
                    hh, b, u = at(h, c, 2)
                    if live(u, N):
                        wait(pe, a_qkT, u + 1)
                        wait(pe, a_exp, 2 * u - 2)
                        s = PS[:, SB + b % 2, 0:384]
                        q, k = qkT[:, b % 2, 0:256], qkT[:, b % 2, 256:512]
                        pe.matmul(s, ident16[:], mask16[:], start=True, stop=False, skip_group_check=True)
                        pe.matmul(s[:, 0:P], q[:, 0:P], k[:, 0:P], start=False, stop=False,
                                  skip_group_check=True)
                        pe.matmul(s[:, P:384], q[:, P:256], k, start=False, stop=True,
                                  skip_group_check=True).then_inc(a_S, 1)
                    hh, b, u = at(h, c, 3)
                    if live(u, N):
                        wait(pe, a_vsb, u)
                        for it in range(2):
                            t = slice(b * S + it * P, b * S + it * P + P)
                            ws = bass.ds(hh * 384 + 256, P)
                            last = mm3(pe, PS[:, VB, it * P:it * P + P],
                                       xT_hi[:, t], xT_lo[:, t], aw_hi[:, ws], aw_lo[:, ws])
                        last.then_inc(a_V, 1)
                        wait(pe, a_prob, 2 * u + 2)
                        wait(pe, a_pT, u)
                        for j in range(3):
                            last = pe.transpose(PS[:, PT, j * P:(j + 1) * P],
                                                prob[:, b % 2, j * P:(j + 1) * P], ident)
                        last.then_inc(a_PT, 1)
                    hh, b, u = at(h, c, 4)
                    if live(u, N):
                        wait(pe, a_pT, u + 1)
                        wait(pe, a_vsb, u + 1)
                        wait(pe, a_OT, u)
                        pe.matmul(PS[:, OB, 0:256], v_sb[:, b % 2, 0, :], pT[:, b % 2, 0:256],
                                  start=True, stop=False, skip_group_check=True)
                        pe.matmul(PS[:, OB, P:256], v_sb[:, b % 2, 1, :], pT[:, b % 2, 256:384],
                                  start=False, stop=True, skip_group_check=True).then_inc(a_O, 1)
                pipeline(pe, AH, step, 4)

            @block.scalar
            def _(act):
                def step(h, c):
                    hh, b, u = at(h, c, 1)
                    if live(u, N):
                        wait(act, a_T, u + 1)
                        wait(act, a_S, u - 1)
                        act.copy(qkT[:, b % 2, :], bank(TB)).then_inc(a_qkT, 1)
                    hh, b, u = at(h, c, 3)
                    if live(u, N):
                        wait(act, a_O, u - 1)
                        act.wait_ge(a_V, u + 1)
                        act.copy(v_sb[:, b % 2, :, :].rearrange("p a b -> p (a b)"), PS[:, VB, 0:256])\
                           .then_inc(a_vsb, 1)
                        act.wait_ge(a_PT, u + 1)
                        act.copy(pT[:, b % 2, :], PS[:, PT, 0:384]).then_inc(a_pT, 1)
                    hh, b, u = at(h, c, 4)
                    if live(u, N):
                        act.wait_ge(a_O, u + 1)
                        act.wait_ge(in_const, 32)
                        act.copy(OT[:, hh, b * S:(b + 1) * S], PS[:, OB, 0:256]).then_inc(a_OT, 1)
                    hh, b, u = at(h, c, 2)
                    if live(u, N):
                        act.wait_ge(a_max, u + 1)
                        wait(act, a_PT, u - 1)
                        for it in range(2):
                            cols = slice(P * it, P + 256 * it)
                            act.activation(prob[:, b % 2, cols], PS[:, SB + b % 2, cols], ACT.Exp,
                                           bias=nmax[:, b % 2, it:it + 1],
                                           accum_out=den[:, b % 2, it:it + 1])\
                               .then_inc(a_exp, 1)
                pipeline(act, AH, step, 4)

            @block.vector
            def _(dve):
                def step(h, c):
                    hh, b, u = at(h, c, 3)
                    if live(u, N):
                        dve.wait_ge(a_exp, 2 * u + 2)
                        dve.reciprocal(rden[:, b % 2, :], den[:, b % 2, :]).then_inc(a_rden, 1)
                        dve.wait_ge(a_rden, u + 1)
                        for it in range(2):
                            cols = slice(P * it, P + 256 * it)
                            dve.tensor_scalar(prob[:, b % 2, cols], prob[:, b % 2, cols],
                                              rden[:, b % 2, it:it + 1], None, ALU.mult)\
                               .then_inc(a_prob, 1)
                    hh, b, u = at(h, c, 0)
                    if live(u, N):
                        wait(dve, a_sum, u - 1)
                        dve.wait_ge(a_qk, u + 1)
                        qk = bank(QK + c % 2)
                        dve.tensor_tensor(rot[:, b % 2, 0, :], qk, a_rope[:, 0, :], ALU.mult)\
                           .then_inc(a_t1, 1)
                        halves = "p (g a i) -> p g a i"
                        dve.tensor_tensor(rot[:, b % 2, 1, :].rearrange(halves, g=4, a=2),
                                          qk.rearrange(halves, g=4, a=2)[:, :, ::-1, :],
                                          a_rope[:, 1, :].rearrange(halves, g=4, a=2), ALU.mult)\
                           .then_inc(a_t2, 1)
                    hh, b, u = at(h, c, 2)
                    if live(u, N):
                        dve.wait_ge(a_S, u + 1)
                        s = bank(SB + b % 2)
                        dve.tensor_reduce(nmax[:, b % 2, 0:1], s[:, 0:P], AX.X, ALU.max, negate=True)
                        dve.tensor_reduce(nmax[:, b % 2, 1:2], s[:, P:384], AX.X, ALU.max, negate=True)\
                           .then_inc(a_max, 1)
                pipeline(dve, AH, step, 4)

            @block.gpsimd
            def _(pool):
                def step(h, c):
                    hh, b, u = at(h, c, 0)
                    if live(u, N):
                        wait(pool, a_T, u - 1)
                        pool.wait_ge(a_t2, u + 1)
                        pool.tensor_tensor(rot[:, b % 2, 2, :], rot[:, b % 2, 0, :],
                                           rot[:, b % 2, 1, :], ALU.add).then_inc(a_sum, 1)
                pipeline(pool, AH, step, 0)

    m_Y, m_res = sem("m_Y"), sem("m_res")
    with nc.Block() as block:
        @block.tensor
        def _(pe):
            pe.wait_ge(in_fw, 96)
            for t in range(NT):
                for h in range(AH):
                    last = pe.matmul(PS[:, t // 4, (t % 4) * P:(t % 4 + 1) * P],
                                     OT[:, h, t * P:(t + 1) * P], wo[:, h, :],
                                     start=(h == 0), stop=(h == AH - 1))
                last.then_inc(m_Y, 1)
            nt_tensor(pe, CT + NT, CT, norm, NT, 2)

        @block.vector
        def _(dve):
            for j in range(2):
                dve.wait_ge(m_Y, 4 * j + 4)
                dve.tensor_tensor(resid[:, 4 * j:4 * j + 4, :],
                                  bank(j).rearrange("p (t d) -> p t d", t=4),
                                  x_tok[:, 4 * j:4 * j + 4, :], ALU.add).then_inc(m_res, 1)
            dve.wait_ge(m_res, 2)
            ln_vector(dve, CT, resid, x1, NT)
            dve.wait_ge(ln_out, CT + NT)
            ln_vector(dve, CT + NT, x1, norm, NT)
            nt_split(dve, CT, NT, xT_hi, xT_lo)

        @block.scalar
        def _(act):
            nt_scalar(act, CT, NT, 2, V_LAT)

        @block.gpsimd
        def _(pool):
            ln_gpsimd(pool, CT, NT)
            ln_gpsimd(pool, CT + NT, NT)

        @block.sync
        def _(sp):
            sp.wait_ge(m_Y, NT)
            sp.dma_start(wo[:], a["x_wo"]).then_inc(in_fw, 16)

    with ExitStack() as stage:
        wq_hi = sb("wq_hi", [P, 2, P], F32R, stage)
        wq_lo = sb("wq_lo", [P, 2, P], F32R, stage)
        krot = sb("krot", [P, 2, 3, 512], F32, stage)
        kS = sb("kS", [P, 2, 2, SC], F32R, stage)
        qS = sb("qS", [P, 2, 2, 2, S], F32R, stage)
        xv = sb("xv", [P, 4, 4, 2, XD + 1], F32, stage)
        xp = sb("xp", [P, 2, 2, 4, S], F32, stage)
        xrd = sb("xrd", [P, 2, 2, 2], F32, stage)
        xo = sb("xo", [P, 2, 2, 2, XD], F32, stage)
        KV, TB, QB, SB = 0, 2, 3, 4
        kv = PS[:, KV:KV + 2, :].rearrange("p a (s n) -> p (a s) n", n=256)
        N = 4 * HP
        x_ones, x_wq, x_K, x_t1, x_t2, x_sum, x_T, x_khi, x_klo, x_Q, x_qhi, x_qlo = (
            sem(n) for n in ("x_ones", "x_wq", "x_K", "x_t1", "x_t2", "x_sum", "x_T", "x_khi",
                             "x_klo", "x_Q", "x_qhi", "x_qlo"))
        x_S, x_exp, x_clip, x_vsb, x_O, x_rd, x_on, x_OT, x_out = (
            sem(n) for n in ("x_S", "x_exp", "x_clip", "x_vsb", "x_O", "x_rd", "x_on",
                             "x_OT", "x_out"))

        with nc.Block() as block:
            @block.tensor
            def _(pe):
                def step(h, c):
                    hh, b, u = at(h, c, 0)
                    if live(u, N):
                        wait(pe, x_vsb, u)
                        for st in range(4):
                            t = slice((4 * b + st) * P, (4 * b + st + 1) * P)
                            last = mm3(pe, kv[:, st, :], cT_hi[:, t], cT_lo[:, t],
                                       xw_hi[:, hh, 256:512], xw_lo[:, hh, 256:512])
                        last.then_inc(x_K, 1)
                    hh, b, u = at(h, c, 1)
                    if live(u, N):
                        wait(pe, x_sum, 2 * u + 2)
                        wait(pe, x_out, u - 3)
                        wait(pe, x_klo, 2 * u)
                        for st in range(4):
                            last = pe.transpose(PS[:, TB, st * P:(st + 1) * P],
                                                krot[:, b % 2, 2, st * P:(st + 1) * P], ident)
                        last.then_inc(x_T, 1)
                        wait(pe, x_wq, 2 * hh + 2)
                        wait(pe, x_qlo, u)
                        wait(pe, x_on, u - 2)
                        t = slice(b * S, (b + 1) * S)
                        for i in range(2):
                            last = mm3(pe, PS[:, QB, i * S:(i + 1) * S], wq_hi[:, i, :],
                                       wq_lo[:, i, :], xT_hi[:, t], xT_lo[:, t])
                        last.then_inc(x_Q, 1)
                    hh, b, u = at(h, c, 2)
                    if live(u, N):
                        for i in range(2):
                            wait(pe, x_klo, 2 * u + i + 1)
                            if i == 0:
                                wait(pe, x_qlo, u + 1)
                            wait(pe, x_exp, 2 * u + i - 1)
                            for st in range(4):
                                o = PS[:, SB + 2 * i + st // 2, (st % 2) * S:(st % 2 + 1) * S]
                                k = kS[:, b % 2, i, st * P:(st + 1) * P]
                                pe.matmul(o, k, qS[:, b % 2, 0, i, :], start=True, stop=False)
                                last = pe.matmul(o, k, qS[:, b % 2, 1, i, :], start=False, stop=True)
                            last.then_inc(x_S, 1)
                    hh, b, u = at(h, c, 3)
                    if live(u, N):
                        wait(pe, x_clip, 2 * u + 2)
                        wait(pe, x_on, u)
                        wait(pe, x_vsb, u + 1)
                        wait(pe, x_qlo, capped(u + 3, N))
                        for i in range(2):
                            for nt in range(2):
                                for st in range(4):
                                    last = pe.matmul(
                                        PS[:, QB, (2 * nt + i) * (XD + 1):(2 * nt + i + 1) * (XD + 1)],
                                        xp[:, b % 2, i, st, nt * P:(nt + 1) * P],
                                        xv[:, b, st, i, :], start=(st == 0), stop=(st == 3))
                        last.then_inc(x_O, 1)
                    hh, b, u = at(h, c, 4)
                    if live(u, N):
                        wait(pe, x_on, u + 1)
                        wait(pe, x_out, u)
                        wait(pe, x_klo, capped(2 * u + 8, 2 * N))
                        for nt in range(2):
                            last = pe.transpose(PS[:, TB, nt * P:(nt + 1) * P],
                                                xo[:, b % 2, nt, :, :], ident)
                        last.then_inc(x_OT, 1)
                pe.wait_ge(x_ones, 1)
                pipeline(pe, HP, step, 4)

            @block.scalar
            def _(act):
                def step(h, c):
                    hh, b, u = at(h, c, 1)
                    if live(u, N):
                        act.wait_ge(x_T, u + 1)
                        wait(act, x_S, 2 * u - 2)
                        act.copy(kS[0:64, b % 2, 0, :], PS[0:64, TB, :]).then_inc(x_khi, 1)
                        act.copy(kS[64:128, b % 2, 1, :], PS[64:128, TB, :]).then_inc(x_khi, 1)
                        act.wait_ge(x_Q, u + 1)
                        act.copy(qS[:, b % 2, 0, :, :].rearrange("p i n -> p (i n)"), bank(QB))\
                           .then_inc(x_qhi, 1)
                    hh, b, u = at(h, c, 0)
                    if live(u, N):
                        act.wait_ge(x_t2, u + 1)
                        wait(act, x_O, u - 3)
                        act.copy(xv[:, b, :, :, 0:XD],
                                 kv[:, :, P:2 * P].rearrange("p s (i d) -> p s i d", i=2)).then_inc(x_vsb, 1)
                    hh, b, u = at(h, c, 2)
                    if live(u, N):
                        wait(act, x_O, u - 1)
                        for i in range(2):
                            act.wait_ge(x_S, 2 * u + i + 1)
                            act.activation(xp[:, b % 2, i, :, :].rearrange("p s n -> p (s n)"),
                                           PS[:, SB + 2 * i:SB + 2 * i + 2, :].rearrange("p a n -> p (a n)"),
                                           ACT.Exp, scale=XD ** -0.5).then_inc(x_exp, 1)
                    hh, b, u = at(h, c, 4)
                    if live(u, N):
                        act.wait_ge(x_OT, u + 1)
                        act.wait_ge(in_const, 32)
                        act.copy(OT[:, hh, b * S:(b + 1) * S], PS[:, TB, 0:S]).then_inc(x_out, 1)
                pipeline(act, HP, step, 4)

            @block.vector
            def _(dve):
                dve.memset(xv[:, :, :, :, XD:XD + 1], 1.0).then_inc(x_ones, 1)

                def step(h, c):
                    hh, b, u = at(h, c, 4)
                    if live(u, N):
                        dve.wait_ge(x_O, u + 1)
                        o = PS[:, QB, 0:4 * (XD + 1)].rearrange("p (g d) -> p g d", g=4)
                        dve.reciprocal(xrd[:, b % 2, :, :].rearrange("p a b -> p (a b)"), o[:, :, XD])\
                           .then_inc(x_rd, 1)
                        dve.wait_ge(x_rd, u + 1)
                        wait(dve, x_OT, u - 1)
                        dve.tensor_tensor(
                            xo[:, b % 2, :, :, :].rearrange("p a b d -> p (a b) d"), o[:, :, 0:XD],
                            xrd[:, b % 2, :, :].rearrange("p a b -> p (a b)").unsqueeze(2)
                            .to_broadcast([P, 4, XD]), ALU.mult).then_inc(x_on, 1)
                    hh, b, u = at(h, c, 0)
                    if live(u, N):
                        wait(dve, x_sum, 2 * u - 2)
                        dve.wait_ge(x_K, u + 1)
                        k = kv[:, :, 0:P]
                        dve.tensor_tensor(krot[:, b % 2, 0, :].rearrange("p (s n) -> p s n", s=4), k,
                                          x_rope[:, 0, :].rearrange("p (s n) -> p s n", s=4), ALU.mult)\
                           .then_inc(x_t1, 1)
                        halves = "p (s a i) -> p s a i"
                        dve.tensor_tensor(krot[:, b % 2, 1, :].rearrange(halves, s=4, a=2),
                                          k.rearrange("p s (a i) -> p s a i", a=2)[:, :, ::-1, :],
                                          x_rope[:, 1, :].rearrange(halves, s=4, a=2), ALU.mult)\
                           .then_inc(x_t2, 1)
                    hh, b, u = at(h, c, 1)
                    if live(u, N):
                        dve.wait_ge(x_khi, 2 * u + 1)
                        dve.tensor_tensor(kS[64:128, b % 2, 0, :], PS[0:64, TB, :],
                                          kS[0:64, b % 2, 0, :].bitcast(F32), ALU.subtract)\
                           .then_inc(x_klo, 1)
                        dve.wait_ge(x_khi, 2 * u + 2)
                        dve.tensor_tensor(kS[0:64, b % 2, 1, :], PS[64:128, TB, :],
                                          kS[64:128, b % 2, 1, :].bitcast(F32), ALU.subtract)\
                           .then_inc(x_klo, 1)
                        dve.wait_ge(x_qhi, u + 1)
                        dve.tensor_tensor(qS[:, b % 2, 1, :, :].rearrange("p i n -> p (i n)"), bank(QB),
                                          qS[:, b % 2, 0, :, :].rearrange("p i n -> p (i n)").bitcast(F32),
                                          ALU.subtract).then_inc(x_qlo, 1)
                    hh, b, u = at(h, c, 2)
                    if live(u, N):
                        for i in range(2):
                            dve.wait_ge(x_exp, 2 * u + i + 1)
                            p = xp[:, b % 2, i, :, :].rearrange("p s n -> p (s n)")
                            dve.tensor_scalar(p, p, CLIP_LO, CLIP_HI, ALU.max, ALU.min)\
                               .then_inc(x_clip, 1)
                pipeline(dve, HP, step, 4)

            @block.gpsimd
            def _(pool):
                def stage_wq(hh, g):
                    wait(pool, x_Q, 4 * g)
                    pool.wait_ge(p_xwlo, HP)
                    for dst, src in ((wq_hi, xw_hi), (wq_lo, xw_lo)):
                        pool.tensor_copy(dst[:].rearrange("p i n -> p (i n)"),
                                         src[:, hh, 0:256].bitcast(F32)).then_inc(x_wq, 1)

                def step(h, c):
                    hh, b, u = at(h, c, 0)
                    if live(u, N):
                        if c == 0:
                            stage_wq(hh, hh)
                        wait(pool, x_T, u - 1)
                        pool.wait_ge(x_t2, u + 1)
                        for i in range(2):
                            t1, t2 = (krot[:, b % 2, j, :].rearrange("p (s a h i) -> p s a h i", s=4, a=2, h=2)
                                      [:, :, :, i, :] for j in range(2))
                            o = krot[:, b % 2, 2, :].rearrange("p (s h a i) -> p s h a i", s=4, a=2, h=2)
                            pool.tensor_tensor(o[:, :, i, :, :], t1, t2, ALU.add).then_inc(x_sum, 1)
                pipeline(pool, HP, step, 0)


    cross.close()
    experts = sb("experts", [P, E, N_EXP])
    gT = sb("gT", [2 * E, T], F32R)
    sel = sb("sel", [2 * E, E, P], F32R)
    accT = sb("accT", [P, T])
    gateb = OT

    m2_Y, m2_res, m2_bo = sem("m2_Y"), sem("m2_res"), sem("m2_bo")
    f_whi, f_wlo, f_P, f_F, f_r, f_G, f_st, f_Vp, f_v, f_vones = (sem(n) for n in (
        "f_whi", "f_wlo", "f_P", "f_F", "f_r", "f_G", "f_st", "f_Vp", "f_v", "f_vones"))
    with ExitStack() as stage:
        qk_st = sb("qk_st", [P, 2, NQ, T], F32R, stage)
        fv = sb("fv", [P, NT, FH, 32], F32, stage)
        fo = x1

        with ExitStack() as early:
            fw_hi = sb("fw_hi", [P, 2 * NQ * P], F32R, early)
            fw_lo = sb("fw_lo", [P, 2 * NQ * P], F32R, early)
            fv_hi = sb("fv_hi", [P, D], F32R, early)
            fv_lo = sb("fv_lo", [P, D], F32R, early)
            bv4 = sb("bv4", [P, 4 * FH, FD], F32, early)
            pf = featT[:, T:2 * T].rearrange("p (a n) -> p a n", a=2)
            pr = sb("pr", [P, 2, 512], F32R, early)
            pg = norm[:, NT:2 * NT, :].rearrange("p (a t) d -> p a (t d)", a=2)
            with nc.Block() as block:
                @block.tensor
                def _(pe):
                    pe.wait_ge(in_fw, 112)
                    for t in range(NT):
                        for h in range(HP):
                            last = pe.matmul(PS[:, t // 4, (t % 4) * P:(t % 4 + 1) * P],
                                             OT[:, h, t * P:(t + 1) * P], wo[:, h, :],
                                             start=(h == 0), stop=(h == HP - 1))
                        last.then_inc(m2_Y, 1)
                    nt_tensor(pe, CT + 3 * NT, CT + NT, norm, NT, 2)
                    pe.wait_ge(f_wlo, 2)
                    for g in range(4 * NQ):
                        n, w = g % 2, g // 2
                        pe.wait_ge(nt_lo, CT + NT + 4 * n + 4)
                        wait(pe, f_F, g - 3)
                        c = slice(n * 512, (n + 1) * 512)
                        mm3(pe, bank(4 + g % 4), fw_hi[:, w * P:(w + 1) * P], fw_lo[:, w * P:(w + 1) * P],
                            xT_hi[:, c], xT_lo[:, c]).then_inc(f_P, 1)
                    for t in range(NT):
                        c = slice(t * P, (t + 1) * P)
                        mm3(pe, PS[:, t // 4, (t % 4) * P:(t % 4 + 1) * P], xT_hi[:, c], xT_lo[:, c],
                            fv_hi[:], fv_lo[:]).then_inc(f_Vp, 1)

                @block.vector
                def _(dve):
                    for j in range(2):
                        ts = slice(4 * j, 4 * j + 4)
                        dve.wait_ge(m2_Y, 4 * j + 4)
                        dve.tensor_tensor(resid[:, ts, :], bank(j).rearrange("p (t d) -> p t d", t=4),
                                          x1[:, ts, :], ALU.add).then_inc(m2_res, 1)
                        dve.wait_ge(m2_res, j + 1)
                        dve.tensor_tensor(resid[:, ts, :], resid[:, ts, :],
                                          rows[:, 0:1, :].to_broadcast([P, 4, D]), ALU.add)\
                           .then_inc(m2_bo, 1)
                    dve.wait_ge(m2_bo, 2)
                    ln_vector(dve, CT + 2 * NT, resid, x2, NT)
                    dve.wait_ge(ln_out, CT + 3 * NT)
                    ln_vector(dve, CT + 3 * NT, x2, norm, NT)
                    nt_split(dve, CT + NT, NT, xT_hi, xT_lo)
                    dve.memset(fv[:, :, :, FD:], 0.0).then_inc(f_vones, 1)
                    dve.wait_ge(f_vones, 1)
                    dve.memset(fv[:, :, :, FD:FD + 1], 1.0).then_inc(f_vones, 1)
                    for g in range(4 * NQ):
                        n, w = g % 2, g // 2
                        ab = C_AB + 2 * (w // NQ)
                        dve.wait_ge(f_F, g + 1)
                        dve.tensor_copy(pr[:, g % 2, :], pf[:, g % 2, :]).then_inc(f_r, 1)
                        dve.wait_ge(f_r, g + 1)
                        dve.tensor_scalar(pg[:, g % 2, :], pr[:, g % 2, :].bitcast(F32),
                                          const[:, ab + 1:ab + 2], None, ALU.mult).then_inc(f_G, 1)
                        dve.wait_ge(f_G, g + 1)
                        dve.scalar_tensor_tensor(qk_st[:, w // NQ, w % NQ, n * 512:(n + 1) * 512],
                                                 pf[:, g % 2, :], const[:, ab:ab + 1], pg[:, g % 2, :],
                                                 ALU.mult, ALU.add).then_inc(f_st, 1)
                    for j in range(2):
                        dve.wait_ge(f_Vp, 4 * j + 4)
                        dve.tensor_tensor(
                            fv[:, 4 * j:4 * j + 4, :, 0:FD].rearrange("p t h d -> p (t h) d"),
                            bank(j).rearrange("p (t d) -> p t d", d=FD),
                            bv4[:], ALU.add).then_inc(f_v, 1)

                @block.scalar
                def _(act):
                    nt_scalar(act, CT + NT, NT, 2, V_LN1)
                    for g in range(4 * NQ):
                        w = g // 2
                        act.wait_ge(f_P, g + 1)
                        wait(act, f_st, g - 1)
                        act.activation(pf[:, g % 2, :], bank(4 + g % 4), ACT.Identity,
                                       bias=vec[:, V_BQK + w:V_BQK + w + 1]).then_inc(f_F, 1)

                @block.sync
                def _(sp):
                    for e in range(E):
                        sp.dma_start(experts[:, e, :], a["experts"][e]).then_inc(in_ex, 16)

                @block.gpsimd
                def _(pool):
                    pool.tensor_copy(fw_hi[:], f_wqk[:]).then_inc(f_whi, 1)
                    pool.tensor_copy(fv_hi[:], f_wvo[:, 0, :]).then_inc(f_whi, 1)
                    for t in range(4):
                        pool.tensor_copy(bv4[:, 16 * t:16 * t + 16, :],
                                         rows[:, 2, :].rearrange("p (h d) -> p h d", d=FD)).then_inc(f_whi, 1)
                    pool.wait_ge(f_whi, 6)
                    pool.tensor_tensor(fw_lo[:], f_wqk[:], fw_hi[:].bitcast(F32), ALU.subtract)\
                        .then_inc(f_wlo, 1)
                    pool.tensor_tensor(fv_lo[:], f_wvo[:, 0, :], fv_hi[:].bitcast(F32), ALU.subtract)\
                        .then_inc(f_wlo, 1)
                    ln_gpsimd(pool, CT + 2 * NT, NT)
                    ln_gpsimd(pool, CT + 3 * NT, NT)

        PT, OB = 4, 7
        N = 4 * NQ
        attn = ExitStack()
        fs = sb("fs", [P, 2, 4, 3 * P], F32, attn)
        fmx = sb("fmx", [P, 2, 2, 4], F32, attn)
        fpT = sb("fpT", [P, 2, 12, P], F32, attn)
        frd = sb("frd", [P, 2, 8], F32, attn)
        foT = featT[:, 0:2 * S].rearrange("p (a n) -> p a n", a=2)
        c_S, c_max, c_sub, c_exp, c_PT, c_pT, c_O, c_oT, c_OT, c_rd, c_on = (sem(n) for n in (
            "c_S", "c_max", "c_sub", "c_exp", "c_PT", "c_pT", "c_O", "c_oT", "c_OT", "c_rd", "c_on"))
        with nc.Block() as block:
            @block.tensor
            def _(pe):
                for k in range(N + 2):
                    u = k
                    if u < N:
                        q, b = u // 4, u % 4
                        for pair in range(2):
                            wait(pe, c_sub, 4 * (u - 1) + 2 * pair + 2)
                            for hh in (2 * pair, 2 * pair + 1):
                                pe.matmul(PS[:, hh, 0:384], ident16[:], mask16[:], start=True,
                                          stop=False, skip_group_check=True)
                            for hh in (2 * pair, 2 * pair + 1):
                                r = slice(32 * hh, 32 * hh + 32)
                                qs, ks = qk_st[r, 0, q, :], qk_st[r, 1, q, :]
                                pe.matmul(PS[:, hh, 0:P], qs[:, b * S:b * S + P], ks[:, b * S:b * S + P],
                                          start=False, stop=False, skip_group_check=True)
                                last = pe.matmul(PS[:, hh, P:384], qs[:, b * S + P:b * S + 2 * P],
                                                 ks[:, b * S:(b + 1) * S], start=False, stop=True,
                                                 skip_group_check=True)
                            last.then_inc(c_S, 1)
                    u = k - 1
                    if 0 <= u < N:
                        pe.wait_ge(c_exp, u + 1)
                        wait(pe, c_pT, u)
                        for j in range(12):
                            last = pe.transpose(PS[:, PT + j // 4, (j % 4) * P:(j % 4 + 1) * P],
                                                fs[:, u % 2, j // 3, (j % 3) * P:(j % 3 + 1) * P], ident)
                        last.then_inc(c_PT, 1)
                    u = k - 2
                    if 0 <= u < N:
                        q, b = u // 4, u % 4
                        pe.wait_ge(c_pT, u + 1)
                        wait(pe, c_on, u)
                        for hh in range(4):
                            v = fv[:, 2 * b:2 * b + 2, 4 * q + hh, :]
                            o = PS[32 * hh:32 * hh + 32, OB, 0:S]
                            pe.matmul(o, v[:, 0, :], fpT[:, u % 2, 3 * hh:3 * hh + 2, :],
                                      start=True, stop=False, skip_group_check=True)
                            last = pe.matmul(o[:, P:S], v[:, 1, :], fpT[:, u % 2, 3 * hh + 2, :],
                                             start=False, stop=True, skip_group_check=True)
                        last.then_inc(c_O, 1)
                        pe.wait_ge(c_oT, u + 1)
                        for it in range(2):
                            last = pe.transpose(PS[:, OB, it * P:(it + 1) * P],
                                                foT[:, u % 2, it * P:(it + 1) * P], ident)
                        last.then_inc(c_OT, 1)

            @block.vector
            def _(dve):
                for k in range(N + 3):
                    u = k - 3
                    if 0 <= u < N:
                        q, b = u // 4, u % 4
                        dve.wait_ge(c_OT, u + 1)
                        o = PS[:, OB, 0:S].rearrange("p (g d) -> p g d", d=32)
                        dve.reciprocal(frd[:, u % 2, :], o[:, :, FD]).then_inc(c_rd, 1)
                        dve.wait_ge(c_rd, u + 1)
                        dve.tensor_tensor(
                            fo[:, 2 * b:2 * b + 2, 32 * q:32 * q + 32].rearrange("p t (h d) -> p t h d", d=FD),
                            o[:, :, 0:FD].rearrange("p (t h) d -> p t h d", t=2),
                            frd[:, u % 2, :].rearrange("p (t h) -> p t h", t=2).unsqueeze(3)
                            .to_broadcast([P, 2, 4, FD]), ALU.mult).then_inc(c_on, 1)
                    u = k
                    if u < N:
                        for pair in range(2):
                            hs = slice(2 * pair, 2 * pair + 2)
                            dve.wait_ge(c_S, 2 * u + pair + 1)
                            for it in range(2):
                                cols = slice(P * it, P + 256 * it)
                                dve.tensor_reduce(fmx[:, u % 2, it, hs], PS[:, hs, cols], AX.X, ALU.max)\
                                   .then_inc(c_max, 1)
                            wait(dve, c_PT, u - 1)
                            for it in range(2):
                                cols = slice(P * it, P + 256 * it)
                                dve.wait_ge(c_max, 4 * u + 2 * pair + it + 1)
                                dve.tensor_tensor(
                                    fs[:, u % 2, hs, cols], PS[:, hs, cols],
                                    fmx[:, u % 2, it, hs].unsqueeze(2).to_broadcast([P, 2, P + P * it]),
                                    ALU.subtract).then_inc(c_sub, 1)

            @block.scalar
            def _(act):
                for k in range(N + 2):
                    u = k - 1
                    if 0 <= u < N:
                        act.wait_ge(c_PT, u + 1)
                        wait(act, c_O, u - 1)
                        act.copy(fpT[:, u % 2, :, :].rearrange("p a b -> p (a b)"),
                                 PS[:, PT:PT + 3, :].rearrange("p a b -> p (a b)")).then_inc(c_pT, 1)
                    u = k
                    if u < N:
                        act.wait_ge(c_sub, 4 * u + 4)
                        e = fs[:, u % 2, :, :].rearrange("p a b -> p (a b)")
                        act.activation(e, e, ACT.Exp, scale=FD ** -0.5).then_inc(c_exp, 1)
                    u = k - 2
                    if 0 <= u < N:
                        act.wait_ge(c_O, u + 1)
                        wait(act, c_OT, u - 1)
                        act.copy(foT[:, u % 2, :], PS[:, OB, 0:S]).then_inc(c_oT, 1)

        attn.close()

        with ExitStack() as early:
            oT = featT[:, T:2 * T]
            x3 = norm[:, NT:2 * NT, :]
            gl = sb("gl", [P, NT, E], F32, early)
            top = sb("top", [P, NT, 8], F32, early)
            topi = sb("topi", [P, NT, 8], U32, early)
            topf = sb("topf", [P, NT, 2], F32, early)
            gw = sb("gw", [P, 4, NT], F32, early)
            g1 = sb("g1", [P, NT, E], F32, early)
            g2 = sb("g2", [P, NT, E], F32, early)
            gates = sb("gates", [P, NT, E], F32, early)
            ghi = sb("ghi", [P, NT, E], F32R, early)
            gparts = sb("gparts", [P, NT, 2, E], F32, early)
            d_T, d_foT, d_Y, d_r1, d_x3, d_r2, d_G, d_gl, d_top, d_ti, d_tf, d_w, d_e, d_gs = (
                sem(n) for n in ("d_T", "d_foT", "d_Y", "d_r1", "d_x3", "d_r2", "d_G", "d_gl",
                                 "d_top", "d_ti", "d_tf", "d_w", "d_e", "d_gs"))
            d_hi, d_parts, d_gT, d_gTs, d_B, d_acc, d_bc, d_Gs, d_sel = (sem(n) for n in (
                "d_hi", "d_parts", "d_gT", "d_gTs", "d_B", "d_acc", "d_bc", "d_Gs", "d_sel"))
            with nc.Block() as block:
                @block.tensor
                def _(pe):
                    for t in range(NT):
                        pe.transpose(PS[:, t // 4, (t % 4) * P:(t % 4 + 1) * P], fo[:, t, :], ident)\
                          .then_inc(d_T, 1)
                    for t in range(NT):
                        pe.wait_ge(d_foT, t // 4 + 1)
                        pe.matmul(PS[:, 2 + t // 4, (t % 4) * P:(t % 4 + 1) * P],
                                  oT[:, t * P:(t + 1) * P], f_wvo[:, 1, :], start=True, stop=True)\
                          .then_inc(d_Y, 1)
                    nt_tensor(pe, CT + 4 * NT, CT + 2 * NT, norm, NT, 4)
                    for t in range(NT):
                        pe.wait_ge(nt_act, CT + 2 * NT + 4 * (t // 4) + 4)
                        pe.matmul(PS[:, 6, t * E:(t + 1) * E], featT[:, t * P:(t + 1) * P], gate_w[:],
                                  start=True, stop=True).then_inc(d_G, 1)
                    pe.wait_ge(d_parts, 2)
                    for t in range(NT):
                        pe.transpose(PS[0:2 * E, t // 4, (t % 4) * P:(t % 4 + 1) * P],
                                     gparts[:, t, :, :], ident).then_inc(d_gT, 1)
                    for n in range(2):
                        pe.wait_ge(d_gTs, n + 1)
                        pe.matmul(bank(2 + n), fc2_b[:], gT[:, n * 512:(n + 1) * 512].bitcast(F32),
                                  start=True, stop=True).then_inc(d_B, 1)
                    pe.wait_ge(d_sel, 1)
                    for g in range(2 * E):
                        e, n = g // 2, g % 2
                        wait(pe, d_Gs, g - 1)
                        if g < 2:
                            pe.wait_ge(nt_act, CT + 3 * NT)
                        pe.matmul(bank(4 + g % 2), sel[:, e, :], gT[:, n * 512:(n + 1) * 512],
                                  start=True, stop=True).then_inc(d_bc, 1)

                @block.scalar
                def _(act):
                    for j in range(2):
                        act.wait_ge(d_T, 4 * j + 4)
                        act.copy(oT[:, j * 512:(j + 1) * 512], bank(j)).then_inc(d_foT, 1)
                    nt_scalar(act, CT + 2 * NT, NT, 4, V_LN2)
                    act.wait_ge(d_w, 1)
                    act.activation(gw[:, 1, :], gw[:, 0, :], ACT.Exp).then_inc(d_e, 1)
                    for j in range(2):
                        act.wait_ge(d_gT, 4 * j + 4)
                        act.copy(gT[:, j * 512:(j + 1) * 512], PS[0:2 * E, j, :]).then_inc(d_gTs, 1)
                    for n in range(2):
                        act.wait_ge(d_B, n + 1)
                        act.copy(accT[:, n * 512:(n + 1) * 512], bank(2 + n)).then_inc(d_acc, 1)
                    for g in range(2 * E):
                        act.wait_ge(d_bc, g + 1)
                        act.copy(gateb[:, g // 2, (g % 2) * 512:(g % 2 + 1) * 512], bank(4 + g % 2))\
                           .then_inc(d_Gs, 1)

                @block.gpsimd
                def _(pool):
                    pool.tensor_copy(sel[:].rearrange("p e m -> p (e m)"), const[0:2 * E, C_SEL:C_SEL + E * P])\
                        .then_inc(d_sel, 1)
                    ln_gpsimd(pool, CT + 4 * NT, NT)
                    pool.wait_ge(d_x3, 2)
                    pool.tensor_tensor(resid[:], x2[:], x3, ALU.add).then_inc(d_r2, 1)

                @block.vector
                def _(dve):
                    for j in range(2):
                        ts = slice(4 * j, 4 * j + 4)
                        dve.wait_ge(d_Y, 4 * j + 4)
                        dve.tensor_tensor(x3[:, ts, :], bank(2 + j).rearrange("p (t d) -> p t d", t=4),
                                          x2[:, ts, :], ALU.add).then_inc(d_r1, 1)
                        dve.wait_ge(d_r1, j + 1)
                        dve.tensor_tensor(x3[:, ts, :], x3[:, ts, :],
                                          rows[:, 1:2, :].to_broadcast([P, 4, D]), ALU.add)\
                           .then_inc(d_x3, 1)
                    dve.wait_ge(d_x3, 2)
                    ln_vector(dve, CT + 4 * NT, x3, norm, NT)
                    nt_split(dve, CT + 2 * NT, NT, xT_hi, xT_lo)
                    dve.wait_ge(d_G, NT)
                    dve.tensor_copy(gl[:].rearrange("p t e -> p (t e)"), PS[:, 6, 0:NT * E]).then_inc(d_gl, 1)
                    dve.wait_ge(d_gl, 1)
                    for t in range(NT):
                        dve.max(out=top[:, t, :], in_=gl[:, t, :]).then_inc(d_top, 1)
                    for t in range(NT):
                        dve.wait_ge(d_top, t + 1)
                        dve.max_index(out=topi[:, t, :], in_max=top[:, t, :], in_values=gl[:, t, :])\
                           .then_inc(d_ti, 1)
                    dve.tensor_tensor(gw[:, 0, :], top[:, :, 1], top[:, :, 0], ALU.subtract).then_inc(d_w, 1)
                    dve.wait_ge(d_ti, NT)
                    dve.tensor_copy(topf[:], topi[:, :, 0:2]).then_inc(d_tf, 1)
                    dve.wait_ge(d_e, 1)
                    dve.tensor_scalar(gw[:, 3, :], gw[:, 1, :], 1.0, None, ALU.add).then_inc(d_w, 1)
                    dve.wait_ge(d_w, 2)
                    dve.reciprocal(gw[:, 2, :], gw[:, 3, :]).then_inc(d_w, 1)
                    dve.wait_ge(d_w, 3)
                    dve.tensor_tensor(gw[:, 3, :], gw[:, 1, :], gw[:, 2, :], ALU.mult).then_inc(d_w, 1)
                    dve.wait_ge(d_w, 4)
                    dve.wait_ge(d_tf, 1)
                    for t in range(NT):
                        for i, g in enumerate((g1, g2)):
                            dve.tensor_scalar(g[:, t, :], const[:, C_IOTA:C_IOTA + E], topf[:, t, i:i + 1],
                                              gw[:, 2 + i, t:t + 1], ALU.is_equal, ALU.mult).then_inc(d_gs, 1)
                    dve.wait_ge(d_gs, 2 * NT)
                    dve.tensor_tensor(gates[:], g1[:], g2[:], ALU.add).then_inc(d_gs, 1)
                    dve.wait_ge(d_gs, 2 * NT + 1)
                    dve.tensor_copy(ghi[:], gates[:]).then_inc(d_hi, 1)
                    dve.wait_ge(d_hi, 1)
                    dve.tensor_copy(gparts[:, :, 0, :], ghi[:].bitcast(F32)).then_inc(d_parts, 1)
                    dve.tensor_tensor(gparts[:, :, 1, :], gates[:], ghi[:].bitcast(F32), ALU.subtract)\
                       .then_inc(d_parts, 1)

    with ExitStack() as stage:
        w_hi = sb("w_hi", [P, 2, 2 * FF], F32R, stage)
        w_lo = sb("w_lo", [P, 2, 2 * FF], F32R, stage)
        b1 = sb("b1", [P, 2, FT], F32, stage)
        hf = sb("hf", [P, 4, 512], F32, stage)
        h_hi = sb("h_hi", [P, 4, 512], F32R, stage)
        h_lo = sb("h_lo", [P, 4, 512], F32R, stage)
        yg = sb("yg", [P, 2, 512], F32, stage)
        outt = sb("outt", [P, NT, D], F32, stage)
        e_whi, e_wlo, e_b1, e_H, e_gelu, e_hi, e_lo, e_Y, e_yg, e_acc = (sem(n) for n in (
            "e_whi", "e_wlo", "e_b1", "e_H", "e_gelu", "e_hi", "e_lo", "e_Y", "e_yg", "e_acc"))
        HB, YB = 0, 4
        NG = 8 * E

        def experts_loop(eng, step):
            for s in range(16):
                step(0, s)
            with eng.Fori(1, E // 2 - 1) as i:
                for s in range(16):
                    step(i, s)
            for s in range(18):
                step(E // 2 - 1, s)

        with nc.Block() as block:
            @block.tensor
            def _(pe):
                def step(i, s):
                    if s < 16:
                        g, p, n, ft = 16 * i + s, s // 8, s % 8 // 4, s % 4
                        if s % 8 == 0:
                            pe.wait_ge(e_wlo, 2 * i + p + 1)
                        wait(pe, e_gelu, g - 3)
                        c = slice(n * 512, (n + 1) * 512)
                        w = slice(ft * P, (ft + 1) * P)
                        mm3(pe, bank(HB + ft), w_hi[:, p, w], w_lo[:, p, w], xT_hi[:, c], xT_lo[:, c])\
                            .then_inc(e_H, 1)
                    if s < 2 and isinstance(i, int) and i == 0:
                        return
                    g, r = 16 * i + s - 2, (s - 2) % 16
                    p, n, ft = r // 8, r % 8 // 4, r % 4
                    wait(pe, e_lo, g + 1)
                    if ft == 0:
                        wait(pe, e_yg, 4 * i + (s - 2) // 4 - 1)
                    w = slice(FF + ft * P, FF + (ft + 1) * P)
                    mm3(pe, bank(YB + n), w_hi[:, p, w], w_lo[:, p, w], h_hi[:, ft, :], h_lo[:, ft, :],
                        start=(ft == 0), stop=(ft == FT - 1)).then_inc(e_Y, 1)
                experts_loop(pe, step)

            @block.scalar
            def _(act):
                def step(i, s):
                    if s >= 16:
                        return
                    g, p, ft = 16 * i + s, s // 8, s % 4
                    wait(act, e_lo, g - 3)
                    if s % 8 == 0:
                        wait(act, e_b1, 2 * i + p + 1)
                    act.wait_ge(e_H, g + 1)
                    act.activation(hf[:, ft, :], bank(HB + ft), ACT.Gelu, bias=b1[:, p, ft:ft + 1])\
                       .then_inc(e_gelu, 1)
                experts_loop(act, step)

            @block.vector
            def _(dve):
                def load(e, p):
                    wait(dve, e_Y, 8 * (e - 1))
                    wait(dve, e_wlo, e - 1)
                    dve.wait_ge(in_ex, 16 * E)
                    dve.tensor_copy(w_hi[:, p, :], experts[:, e, 0:2 * FF]).then_inc(e_whi, 1)
                    dve.tensor_copy(b1[:, p, :], experts[:, e, WB:WB + FT]).then_inc(e_b1, 1)

                def step(i, s):
                    if s % 8 == 2 and not (isinstance(i, int) and 2 * i + s // 8 + 1 >= E):
                        load(2 * i + s // 8 + 1, (s // 8 + 1) % 2)
                    if s < 17 and not (isinstance(i, int) and 16 * i + s < 1):
                        g, ft = 16 * i + s - 1, (s - 1) % 4
                        wait(dve, e_Y, g - 3)
                        dve.wait_ge(e_gelu, g + 1)
                        dve.tensor_copy(h_hi[:, ft, :], hf[:, ft, :]).then_inc(e_hi, 1)
                        dve.wait_ge(e_hi, g + 1)
                        dve.tensor_tensor(h_lo[:, ft, :], hf[:, ft, :], h_hi[:, ft, :].bitcast(F32),
                                          ALU.subtract).then_inc(e_lo, 1)
                    if (s - 2) % 4 == 3 and not (isinstance(i, int) and i == 0 and s < 2):
                        y, n = 4 * i + (s - 2) // 4, (s - 2) // 4 % 2
                        e = 2 * i + (s - 2) // 8
                        wait(dve, e_acc, y - 1)
                        dve.wait_ge(e_Y, 4 * y + 4)
                        dve.tensor_tensor(yg[:, n, :], bank(YB + n),
                                          gateb[:, e, n * 512:(n + 1) * 512], ALU.mult).then_inc(e_yg, 1)
                load(0, 0)
                experts_loop(dve, step)

            @block.gpsimd
            def _(pool):
                def load(e, p):
                    pool.wait_ge(e_whi, e + 1)
                    pool.wait_ge(in_ex, 16 * E)
                    pool.tensor_tensor(w_lo[:, p, :], experts[:, e, 0:2 * FF], w_hi[:, p, :].bitcast(F32),
                                       ALU.subtract).then_inc(e_wlo, 1)

                def step(i, s):
                    if s % 8 == 2 and not (isinstance(i, int) and 2 * i + s // 8 + 1 >= E):
                        load(2 * i + s // 8 + 1, (s // 8 + 1) % 2)
                    if (s - 2) % 4 == 3 and not (isinstance(i, int) and i == 0 and s < 2):
                        y, n = 4 * i + (s - 2) // 4, (s - 2) // 4 % 2
                        c = slice(n * 512, (n + 1) * 512)
                        wait(pool, e_acc, y - 1)
                        pool.wait_ge(e_yg, y + 1)
                        pool.tensor_tensor(accT[:, c], accT[:, c], yg[:, n, :], ALU.add).then_inc(e_acc, 1)
                load(0, 0)
                experts_loop(pool, step)

        z_T, z_res, z_out = sem("z_T"), sem("z_res"), sem("z_out")
        with nc.Block() as block:
            @block.tensor
            def _(pe):
                for t in range(NT):
                    pe.transpose(PS[:, t // 4, (t % 4) * P:(t % 4 + 1) * P],
                                 accT[:, t * P:(t + 1) * P], ident).then_inc(z_T, 1)

            @block.vector
            def _(dve):
                for j in range(2):
                    ts = slice(4 * j, 4 * j + 4)
                    dve.wait_ge(z_T, 4 * j + 4)
                    dve.tensor_tensor(x1[:, ts, :], bank(j).rearrange("p (t d) -> p t d", t=4),
                                      resid[:, ts, :], ALU.add).then_inc(z_res, 1)
                dve.wait_ge(z_res, 2)
                ln_vector(dve, CT + 5 * NT, x1, outt, NT)

            @block.gpsimd
            def _(pool):
                ln_gpsimd(pool, CT + 5 * NT, NT)

            @block.sync
            def _(sp):
                for j in range(2):
                    sp.wait_ge(ln_out, CT + 5 * NT + 4 * j + 4)
                    sp.dma_start(out[:, 4 * j:4 * j + 4, :], outt[:, 4 * j:4 * j + 4, :]).then_inc(z_out, 16)
                sp.wait_ge(z_out, 32)


def constants():
    c = np.zeros((P, N_CONST), np.float32)
    c[:, C_ID:C_ID + P] = np.eye(P)
    c[:, C_MASK:C_MASK + P] = np.where(np.arange(P)[:, None] < np.arange(P)[None, :], MASKED, 0.0)
    c[:, C_IOTA:C_IOTA + E] = np.arange(E)
    part = np.arange(P) % 32 // FD
    q_low, k_low = part % 2, part // 2
    c[:, C_AB:C_AB + 4] = np.stack([q_low, 1 - 2 * q_low, k_low, 1 - 2 * k_low], 1)
    for e in range(E):
        c[[e, E + e], C_SEL + e * P:C_SEL + (e + 1) * P] = 1.0
    half = D // 2
    freq = np.power(np.float32(10000.0), -np.arange(half, dtype=np.float32) / np.float32(half))
    ang = np.arange(S, dtype=np.float32)[:, None] * freq.astype(np.float32)[None, :]
    cos, sin = np.cos(ang), np.sin(ang)
    cos = np.concatenate([cos, cos], 1).reshape(2, P, 1, D)
    sin = np.concatenate([-sin, sin], 1).reshape(2, P, 1, D)
    scale = np.array([1.0 / D, 1.0], np.float32)[None, None, :, None]
    rope = np.stack([np.broadcast_to(t * scale, (2, P, 2, D)) for t in (cos, sin)])
    rope = rope.transpose(2, 0, 1, 3, 4).reshape(P, 2, 512).astype(np.float32)
    return c, rope


def kernel(**x):
    import concourse.bacc as bacc
    from concourse.bass_utils import run_bass_kernel_spmd

    x = {k: np.asarray(v) for k, v in x.items()}

    def tiles(v):
        return v.reshape(-1, P, v.shape[-1]).transpose(1, 0, 2)

    def table(v):
        v = v.reshape(4, P, 1, XD // 2)
        return np.broadcast_to(v, (4, P, 4, XD // 2)).transpose(1, 0, 2, 3).reshape(P, 512)

    xf = x["x"].reshape(T, D)
    wq = x["L0_xattn_Wq"].reshape(D, HP, 2, 1, XD)
    wq = np.broadcast_to(wq, (D, HP, 2, 2, XD)).reshape(D, HP, 256)
    wkv = x["L0_xattn_Wkv"]
    wk = wkv[:, :XH * XD].reshape(D, HP, 2, 2, XD // 2).transpose(0, 1, 3, 2, 4)
    wkv = np.concatenate([wk.reshape(D, HP, P), wkv[:, XH * XD:].reshape(D, HP, P)], 2)
    qk = x["L0_ffn_Wqkv"][:, :2 * D].reshape(D, 2, NQ, 4, 1, FD)
    qk = np.broadcast_to(qk, (D, 2, NQ, 4, 4, FD)).reshape(D, 2 * NQ * P)
    bqk = x["L0_ffn_bqkv"][:2 * D].reshape(2 * NQ, 4, 1, FD)
    bqk = np.broadcast_to(bqk, (2 * NQ, 4, 4, FD)).reshape(2 * NQ, P).T
    fc1 = x["L0_ffn_fc1_w"].transpose(0, 2, 1)
    fc2 = x["L0_ffn_fc2_w"].reshape(E, D, FT, P).transpose(0, 3, 2, 1).reshape(E, P, FT * D)
    fb1 = x["L0_ffn_fc1_b"].reshape(E, FT, P).transpose(0, 2, 1)
    const, a_rope = constants()
    arrays = {
        "const": const,
        "a_rope": a_rope,
        "x_rope": np.stack([table(x["L0_xattn_cos"]), table(x["L0_xattn_sin"])], 1),
        "x_tok": tiles(xf),
        "xT": xf.T,
        "ctx_tok": tiles(x["ctx_1024"].reshape(B * SC, D)),
        "vec": np.concatenate([np.stack([x["L0_xattn_ln_ctx_g"], x["L0_xattn_ln_ctx_b"],
                                         x["L0_xattn_ln_lat_g"], x["L0_xattn_ln_lat_b"],
                                         x["L0_ffn_ln1_w"], x["L0_ffn_ln1_b"],
                                         x["L0_ffn_ln2_w"], x["L0_ffn_ln2_b"]], 1), bqk], 1),
        "rows": np.broadcast_to(np.stack([x["L0_xattn_bo"], x["L0_ffn_bo"],
                                          x["L0_ffn_bqkv"][2 * D:]])[None], (P, 3, D)),
        "a_w": np.concatenate([x["L0_attn_wq"], x["L0_attn_wk"], x["L0_attn_wv"]], 2),
        "a_wo": x["L0_attn_wo"].transpose(1, 0, 2),
        "x_w": np.concatenate([wq, wkv], 2),
        "x_wo": tiles(x["L0_xattn_Wo"]),
        "f_wqk": qk,
        "f_wvo": np.stack([x["L0_ffn_Wqkv"][:, 2 * D:], x["L0_ffn_Wo"]], 1),
        "gate_w": x["L0_ffn_gate_W"],
        "fc2_b": np.concatenate([x["L0_ffn_fc2_b"]] * 2, 0),
        "experts": np.concatenate([fc1, fc2, fb1], 2),
    }
    arrays = {k: np.ascontiguousarray(v) for k, v in arrays.items()}
    nc = bacc.Bacc("TRN2", target_bir_lowering=False, num_devices=1)
    a = {k: nc.dram_tensor("in_" + k, v.shape, mybir.dt.from_np(v.dtype), kind="ExternalInput").ap()
         for k, v in arrays.items()}
    out = nc.dram_tensor("out_dram", (P, NT, D), F32, kind="ExternalOutput").ap()
    build_program(nc, a, out)
    r = run_bass_kernel_spmd(nc, [{"in_" + k: v for k, v in arrays.items()}], core_ids=[0])
    return r.results[0]["out_dram"].transpose(1, 0, 2).reshape(B, S, D)
```

```python
from contextlib import ExitStack

import numpy as np

import concourse.bass as bass
from concourse import mybir

F32 = mybir.dt.float32
F32R = mybir.dt.float32r
BF16 = mybir.dt.bfloat16
U32 = mybir.dt.uint32
ALU = mybir.AluOpType
ACT = mybir.ActivationFunctionType
AX = mybir.AxisListType

P = 128
D = 128
B, S = 4, 256
T = B * S
NT = T // P
SC = 512
CT = B * SC // P
AH = 8
XH, XD = 16, 64
HP = XH // 2
FH, FD = 16, 8
NQ = FH // 4
E, FF = 8, 512
FT = FF // P
EPS = 1e-5
MASKED = -1e30
CLIP_LO, CLIP_HI = float(np.exp(np.float32(-11.0))), float(np.exp(np.float32(11.0)))

C_ID, C_MASK, C_IOTA, C_AB, C_SEL = 0, P, 2 * P, 2 * P + 8, 2 * P + 12
N_CONST = C_SEL + E * P
V_CTX, V_LAT, V_LN1, V_LN2, V_BQK = 0, 2, 4, 6, 8
N_VEC = V_BQK + 2 * NQ
W1, W2, WB = 0, FF, 2 * FF
N_EXP = 2 * FF + FT


def wait(eng, sem, n):
    if not isinstance(n, int) or n > 0:
        eng.wait_ge(sem, n)


def at(h, c, skew):
    h, c = h + (c - skew) // 4, (c - skew) % 4
    return h, c, 4 * h + c


def live(u, n):
    return not isinstance(u, int) or 0 <= u < n


def capped(n, most):
    return min(n, most) if isinstance(n, int) else n


def pipeline(eng, groups, step, skew):
    for k in range(8):
        step(k // 4, k % 4)
    with eng.Fori(2, groups) as h:
        for c in range(4):
            step(h, c)
    for k in range(4 * groups, 4 * groups + skew):
        step(k // 4, k % 4)


def build_program(nc, a, out):
    with ExitStack() as ctx:
        build(nc, ctx, a, out)


def build(nc, ctx, a, out):
    def sb(name, shape, dt=F32, stack=ctx):
        return stack.enter_context(nc.sbuf_tensor(name, shape, dt))

    def sem(name):
        return ctx.enter_context(nc.semaphore(name))

    PS = ctx.enter_context(nc.psum_tensor("PS", [P, 8, 512], F32))

    def bank(i):
        return PS[:, i, :]

    const = sb("const", [P, N_CONST])
    ident = const[:, C_ID:C_ID + P]
    ident16 = sb("ident16", [P, P], BF16)
    mask16 = sb("mask16", [P, 3, P], BF16)
    vec = sb("vec", [P, N_VEC])
    rows = sb("rows", [P, 3, D])
    x_tok = sb("x_tok", [P, NT, D])
    resid = sb("resid", [P, NT, D])
    x1 = sb("x1", [P, NT, D])
    x2 = sb("x2", [P, NT, D])
    lat = resid
    norm = sb("norm", [P, CT, D])
    featT = sb("featT", [P, CT * P])
    stats = sb("stats", [P, CT, 6])
    mv = sb("mv", [P, CT, 2])
    rstd = sb("rstd", [P, CT])
    half = sb("half", [P, CT])
    OT = sb("OT", [P, 8, T])
    wo = sb("wo", [P, 8, D])
    f_wqk = sb("f_wqk", [P, 2 * NQ * P])
    f_wvo = sb("f_wvo", [P, 2, D])
    gate_w = sb("gate_w", [P, E])
    fc2_b = sb("fc2_b", [2 * E, D])

    in_const, in_xT, in_x, in_aw, in_ctx, in_xw, in_fw, in_ex = (sem(n) for n in (
        "in_const", "in_xT", "in_x", "in_aw", "in_ctx", "in_xw", "in_fw", "in_ex"))
    ln_raw, ln_stats, ln_eps, ln_rstd, ln_out = (sem(n) for n in (
        "ln_raw", "ln_stats", "ln_eps", "ln_rstd", "ln_out"))
    nt_pe, nt_act, nt_hi, nt_lo = (sem(n) for n in ("nt_pe", "nt_act", "nt_hi", "nt_lo"))

    def ln_statistics(dve, n_ln, src, n, slot=0):
        for t in range(n):
            dve.bn_stats(stats[:, slot + t, :], src[:, t, :]).then_inc(ln_raw, 1)
        for t in range(n):
            dve.wait_ge(ln_raw, n_ln + t + 1)
            dve.bn_aggr(mv[:, slot + t, :], stats[:, slot + t, :]).then_inc(ln_stats, 1)

    def ln_apply(dve, n_ln, src, dst, n, slot=0):
        dve.wait_ge(ln_rstd, n_ln + n)
        for t in range(n):
            dve.tensor_scalar(dst[:, t, :], src[:, t, :], mv[:, slot + t, 0:1],
                              rstd[:, slot + t:slot + t + 1],
                              ALU.subtract, ALU.mult).then_inc(ln_out, 1)

    def ln_gpsimd(pool, n_ln, n, slot=0):
        r = rstd[:, slot:slot + n]
        pool.wait_ge(ln_stats, n_ln + n)
        pool.tensor_scalar(r, mv[:, slot:slot + n, 1], EPS, None, ALU.add).then_inc(ln_eps, n)
        pool.wait_ge(ln_eps, n_ln + n)
        pool.tensor_tensor(r, r, half[:, 0:n], ALU.pow).then_inc(ln_rstd, n)

    def nt_tensor(pe, n_ln, src, n, first_bank):
        for t in range(n):
            pe.wait_ge(ln_out, n_ln + t + 1)
            pe.transpose(PS[:, first_bank + t // 4, (t % 4) * P:(t % 4 + 1) * P],
                         src[:, t, :], ident).then_inc(nt_pe, 1)

    def nt_scalar(act, n_nt, n, first_bank, v, at_bank=0):
        for j in range(n // 4):
            act.wait_ge(nt_pe, n_nt + 4 * j + 4)
            act.activation(featT[:, (at_bank + j) * 512:(at_bank + j + 1) * 512], bank(first_bank + j), ACT.Identity,
                           bias=vec[:, v + 1:v + 2], scale=vec[:, v:v + 1]).then_inc(nt_act, 4)

    def nt_split(dve, n_nt, n, hi, lo):
        for j in range(n // 4):
            c = slice(j * 512, (j + 1) * 512)
            dve.wait_ge(nt_act, n_nt + 4 * j + 4)
            dve.tensor_copy(hi[:, c], featT[:, c]).then_inc(nt_hi, 4)
            dve.wait_ge(nt_hi, n_nt + 4 * j + 4)
            dve.tensor_tensor(lo[:, c], featT[:, c], hi[:, c].bitcast(F32),
                              ALU.subtract).then_inc(nt_lo, 4)

    def mm3(pe, o, w_hi, w_lo, m_hi, m_lo, start=True, stop=True, **kw):
        pe.matmul(o, w_hi, m_hi, start=start, stop=False, **kw)
        pe.matmul(o, w_hi, m_lo, start=False, stop=False, **kw)
        return pe.matmul(o, w_lo, m_hi, start=False, stop=stop, **kw)

    xT_hi = sb("xT_hi", [P, T], F32R)
    xT_lo = sb("xT_lo", [P, T], F32R)
    cross = ExitStack()
    xw_hi = sb("xw_hi", [P, HP, 512], F32R, cross)
    xw_lo = sb("xw_lo", [P, HP, 512], F32R, cross)
    x_rope = sb("x_rope", [P, 2, 512], F32, cross)
    cT_hi = sb("cT_hi", [P, CT * P], F32R, cross)
    cT_lo = sb("cT_lo", [P, CT * P], F32R, cross)

    with ExitStack() as stage:
        xT_raw = OT[:, 6, :]
        aw_raw = sb("aw_raw", [P, AH, 3 * P], F32, stage)
        aw_hi = sb("aw_hi", [P, AH * 3 * P], F32R, stage)
        aw_lo = sb("aw_lo", [P, AH * 3 * P], F32R, stage)
        a_rope = sb("a_rope", [P, 2, 512], F32, stage)
        rot = sb("rot", [P, 2, 3, 512], F32, stage)
        qkT = sb("qkT", [P, 2, 512], F32, stage)
        v_sb = sb("v_sb", [P, 2, 2, P], F32, stage)
        nmax = sb("nmax", [P, 2, 2], F32, stage)
        den = sb("den", [P, 2, 2], F32, stage)
        rden = sb("rden", [P, 2, 2], F32, stage)
        prob = sb("prob", [P, 2, 3 * P], F32, stage)
        pT = sb("pT", [P, 2, 3 * P], F32, stage)

        p_const, p_xhi, p_awhi, p_awlo, p_xwhi, p_sin, p_xwlo = (sem(n) for n in (
            "p_const", "p_xhi", "p_awhi", "p_awlo", "p_xwhi", "p_sin", "p_xwlo"))

        aw = aw_raw[:].rearrange("p h n -> p (h n)")
        AW, AV = 4 * 3 * P, 6 * 3 * P
        p_awhi2, p_awhi3 = sem("p_awhi2"), sem("p_awhi3")

        with nc.Block() as block:
            @block.sync
            def _(sp):
                sp.dma_start(xT_raw, a["xT"]).then_inc(in_xT, 16)
                sp.dma_start(aw_raw[:, AH // 2:, :], a["a_w"][:, AH // 2:, :]).then_inc(in_aw, 16)
                sp.wait_ge(in_xT, 16)
                sp.wait_ge(in_aw, 48)
                sp.dma_start(x_tok[:], a["x_tok"]).then_inc(in_x, 16)
                sp.dma_start(norm[:], a["ctx_tok"]).then_inc(in_ctx, 16)
                sp.dma_start(x_rope[:], a["x_rope"]).then_inc(in_xw, 16)
                sp.dma_start(rows[:], a["rows"]).then_inc(in_fw, 16)
                sp.dma_start(f_wvo[:], a["f_wvo"]).then_inc(in_fw, 16)
                sp.dma_start(gate_w[:], a["gate_w"]).then_inc(in_fw, 16)
                sp.dma_start(fc2_b[:], a["fc2_b"]).then_inc(in_fw, 16)
                sp.dma_start(wo[:], a["a_wo"]).then_inc(in_fw, 16)
                sp.dma_start(f_wqk[:], a["f_wqk"]).then_inc(in_fw, 16)

            @block.scalar
            def _(act):
                act.dma_start(aw_raw[:, :AH // 2, :], a["a_w"][:, :AH // 2, :]).then_inc(in_aw, 16)
                act.dma_start(const[:], a["const"]).then_inc(in_const, 16)
                act.dma_start(vec[:], a["vec"]).then_inc(in_const, 16)
                act.dma_start(a_rope[:], a["a_rope"]).then_inc(in_aw, 16)
                act.wait_ge(in_const, 32)
                act.copy(ident16[:], ident).then_inc(p_const, 1)
                for j in (0, 2):
                    act.copy(mask16[:, j, :], const[:, C_MASK:C_MASK + P]).then_inc(p_const, 1)
                act.wait_ge(in_aw, 48)
                act.copy(aw_hi[:, AV:], aw[:, AV:]).then_inc(p_awhi3, 1)
                act.copy(aw_hi[:, AW:AV], aw[:, AW:AV]).then_inc(p_awhi2, 1)

            @block.gpsimd
            def _(pool):
                pool.memset(half[:], -0.5).then_inc(p_const, 1)
                pool.memset(mask16[:, 1, :], 0.0).then_inc(p_const, 1)
                pool.wait_ge(p_awhi3, 1)
                pool.tensor_tensor(aw_lo[:, AV:], aw[:, AV:], aw_hi[:, AV:].bitcast(F32),
                                   ALU.subtract).then_inc(p_awlo, 1)

            @block.vector
            def _(dve):
                dve.wait_ge(in_xT, 16)
                dve.tensor_copy(xT_hi[:], xT_raw).then_inc(p_xhi, 1)
                dve.wait_ge(p_xhi, 1)
                dve.tensor_tensor(xT_lo[:], xT_raw, xT_hi[:].bitcast(F32), ALU.subtract)\
                   .then_inc(p_xhi, 1)
                dve.wait_ge(in_aw, 48)
                dve.tensor_copy(aw_hi[:, :AW], aw[:, :AW]).then_inc(p_awhi, 1)
                dve.wait_ge(p_awhi, 1)
                dve.tensor_tensor(aw_lo[:, :AW], aw[:, :AW], aw_hi[:, :AW].bitcast(F32),
                                  ALU.subtract).then_inc(p_awlo, 1)
                dve.wait_ge(p_awhi2, 1)
                dve.tensor_tensor(aw_lo[:, AW:AV], aw[:, AW:AV], aw_hi[:, AW:AV].bitcast(F32),
                                  ALU.subtract).then_inc(p_awlo, 1)

        QK, TB, SB, PT, VB, OB = 0, 2, 3, 5, 6, 7
        N = 4 * AH
        a_qk, a_t1, a_t2, a_sum, a_T, a_qkT, a_S, a_max, a_exp, a_rden, a_prob = (sem(n) for n in (
            "a_qk", "a_t1", "a_t2", "a_sum", "a_T", "a_qkT", "a_S", "a_max", "a_exp", "a_rden",
            "a_prob"))
        a_V, a_vsb, a_PT, a_pT, a_O, a_OT = (sem(n) for n in (
            "a_V", "a_vsb", "a_PT", "a_pT", "a_O", "a_OT"))

        with nc.Block() as block:
            @block.tensor
            def _(pe):
                def step(h, c):
                    hh, b, u = at(h, c, 0)
                    if live(u, N):
                        wait(pe, a_t2, u - 1)
                        for it in range(2):
                            t = slice(b * S + it * P, b * S + it * P + P)
                            ws = bass.ds(hh * 384, 256)
                            last = mm3(pe, PS[:, QK + c % 2, it * 256:it * 256 + 256],
                                       xT_hi[:, t], xT_lo[:, t], aw_hi[:, ws], aw_lo[:, ws])
                        last.then_inc(a_qk, 1)
                    hh, b, u = at(h, c, 2)
                    if live(u, N):
                        wait(pe, a_qkT, u + 1)
                        wait(pe, a_exp, 2 * u - 2)
                        s = PS[:, SB + b % 2, 0:384]
                        q, k = qkT[:, b % 2, 0:256], qkT[:, b % 2, 256:512]
                        pe.matmul(s, ident16[:], mask16[:], start=True, stop=False, skip_group_check=True)
                        pe.matmul(s[:, 0:P], q[:, 0:P], k[:, 0:P], start=False, stop=False,
                                  skip_group_check=True)
                        pe.matmul(s[:, P:384], q[:, P:256], k, start=False, stop=True,
                                  skip_group_check=True).then_inc(a_S, 1)
                    hh, b, u = at(h, c, 1)
                    if live(u, N):
                        wait(pe, a_sum, u + 1)
                        wait(pe, a_qkT, u)
                        for j in range(4):
                            src = rot[:, b % 2, 2, :].rearrange("p (t q d) -> p q t d", t=2, q=2)
                            last = pe.transpose(PS[:, TB, j * P:(j + 1) * P],
                                                src[:, j // 2, j % 2, :], ident)
                        last.then_inc(a_T, 1)
                    hh, b, u = at(h, c, 3)
                    if live(u, N):
                        wait(pe, a_vsb, u)
                        for it in range(2):
                            t = slice(b * S + it * P, b * S + it * P + P)
                            ws = bass.ds(hh * 384 + 256, P)
                            last = mm3(pe, PS[:, VB, it * P:it * P + P],
                                       xT_hi[:, t], xT_lo[:, t], aw_hi[:, ws], aw_lo[:, ws])
                        last.then_inc(a_V, 1)
                    hh, b, u = at(h, c, 3)
                    if live(u, N):
                        wait(pe, a_prob, 2 * u + 2)
                        wait(pe, a_pT, u)
                        for j in range(3):
                            last = pe.transpose(PS[:, PT, j * P:(j + 1) * P],
                                                prob[:, b % 2, j * P:(j + 1) * P], ident)
                        last.then_inc(a_PT, 1)
                    hh, b, u = at(h, c, 4)
                    if live(u, N):
                        wait(pe, a_pT, u + 1)
                        wait(pe, a_vsb, u + 1)
                        wait(pe, a_OT, u)
                        pe.matmul(PS[:, OB, 0:256], v_sb[:, b % 2, 0, :], pT[:, b % 2, 0:256],
                                  start=True, stop=False, skip_group_check=True)
                        pe.matmul(PS[:, OB, P:256], v_sb[:, b % 2, 1, :], pT[:, b % 2, 256:384],
                                  start=False, stop=True, skip_group_check=True).then_inc(a_O, 1)
                pipeline(pe, AH, step, 4)

            @block.scalar
            def _(act):
                def step(h, c):
                    hh, b, u = at(h, c, 1)
                    if live(u, N):
                        wait(act, a_T, u + 1)
                        wait(act, a_S, u - 1)
                        act.copy(qkT[:, b % 2, :], bank(TB)).then_inc(a_qkT, 1)
                    hh, b, u = at(h, c, 2)
                    if live(u, N):
                        act.wait_ge(a_max, u + 1)
                        wait(act, a_PT, u - 1)
                        for it in range(2):
                            cols = slice(P * it, P + 256 * it)
                            act.activation(prob[:, b % 2, cols], PS[:, SB + b % 2, cols], ACT.Exp,
                                           bias=nmax[:, b % 2, it:it + 1],
                                           accum_out=den[:, b % 2, it:it + 1])\
                               .then_inc(a_exp, 1)
                    hh, b, u = at(h, c, 3)
                    if live(u, N):
                        wait(act, a_O, u - 1)
                        act.wait_ge(a_V, u + 1)
                        act.copy(v_sb[:, b % 2, :, :].rearrange("p a b -> p (a b)"), PS[:, VB, 0:256])\
                           .then_inc(a_vsb, 1)
                    hh, b, u = at(h, c, 3)
                    if live(u, N):
                        wait(act, a_O, u - 1)
                        act.wait_ge(a_PT, u + 1)
                        act.copy(pT[:, b % 2, :], PS[:, PT, 0:384]).then_inc(a_pT, 1)
                    hh, b, u = at(h, c, 4)
                    if live(u, N):
                        act.wait_ge(a_O, u + 1)
                        act.wait_ge(in_const, 32)
                        act.copy(OT[:, hh, b * S:(b + 1) * S], PS[:, OB, 0:256]).then_inc(a_OT, 1)
                pipeline(act, AH, step, 4)

            @block.vector
            def _(dve):
                def step(h, c):
                    hh, b, u = at(h, c, 3)
                    if live(u, N):
                        dve.wait_ge(a_exp, 2 * u + 2)
                        dve.reciprocal(rden[:, b % 2, :], den[:, b % 2, :]).then_inc(a_rden, 1)
                        dve.wait_ge(a_rden, u + 1)
                        for it in range(2):
                            cols = slice(P * it, P + 256 * it)
                            dve.tensor_scalar(prob[:, b % 2, cols], prob[:, b % 2, cols],
                                              rden[:, b % 2, it:it + 1], None, ALU.mult)\
                               .then_inc(a_prob, 1)
                    hh, b, u = at(h, c, 0)
                    if live(u, N):
                        wait(dve, a_sum, u - 1)
                        dve.wait_ge(a_qk, u + 1)
                        qk = bank(QK + c % 2)
                        dve.tensor_tensor(rot[:, b % 2, 0, :], qk, a_rope[:, 0, :], ALU.mult)\
                           .then_inc(a_t1, 1)
                        halves = "p (g a i) -> p g a i"
                        dve.tensor_tensor(rot[:, b % 2, 1, :].rearrange(halves, g=4, a=2),
                                          qk.rearrange(halves, g=4, a=2)[:, :, ::-1, :],
                                          a_rope[:, 1, :].rearrange(halves, g=4, a=2), ALU.mult)\
                           .then_inc(a_t2, 1)
                    hh, b, u = at(h, c, 2)
                    if live(u, N):
                        dve.wait_ge(a_S, u + 1)
                        s = bank(SB + b % 2)
                        dve.tensor_reduce(nmax[:, b % 2, 0:1], s[:, 0:P], AX.X, ALU.max, negate=True)
                        dve.tensor_reduce(nmax[:, b % 2, 1:2], s[:, P:384], AX.X, ALU.max, negate=True)\
                           .then_inc(a_max, 1)
                pipeline(dve, AH, step, 4)

            @block.gpsimd
            def _(pool):
                def step(h, c):
                    hh, b, u = at(h, c, 0)
                    if live(u, N):
                        wait(pool, a_T, u - 1)
                        pool.wait_ge(a_t2, u + 1)
                        pool.tensor_tensor(rot[:, b % 2, 2, :], rot[:, b % 2, 0, :],
                                           rot[:, b % 2, 1, :], ALU.add).then_inc(a_sum, 1)
                pipeline(pool, AH, step, 0)

    m_Y, m_res = sem("m_Y"), sem("m_res")
    with ExitStack() as stage, nc.Block() as block:
        xw_raw = sb("xw_raw", [P, HP, 512], F32, stage)

        @block.tensor
        def _(pe):
            def product(t):
                for h in range(AH):
                    last = pe.matmul(PS[:, t // 4, (t % 4) * P:(t % 4 + 1) * P],
                                     OT[:, h, t * P:(t + 1) * P], wo[:, h, :],
                                     start=(h == 0), stop=(h == AH - 1))
                last.then_inc(m_Y, 1)
            pe.wait_ge(in_fw, 96)
            for t in range(4):
                product(t)
            for t in range(4, NT):
                product(t)
            nt_tensor(pe, 0, norm, CT, 4)
            for j in range(2):
                nt_tensor(pe, CT + 8 + 4 * j, lat[:, 4 * j:4 * j + 4, :], 4, 2 + j)

        @block.vector
        def _(dve):
            dve.wait_ge(in_ctx, 16)
            ln_statistics(dve, 0, norm, CT)
            ln_apply(dve, 0, norm, norm, CT)
            dve.wait_ge(in_xw, 32)
            for h in range(HP):
                dve.tensor_copy(xw_hi[:, h, :], xw_raw[:, h, :]).then_inc(p_xwhi, 1)
            sin = x_rope[:, 1, :].rearrange("p (s a i) -> p s a i", s=4, a=2)[:, :, 0, :]
            dve.tensor_scalar(sin, sin, -1.0, None, ALU.mult).then_inc(p_sin, 1)
            for j in range(2):
                ts = slice(4 * j, 4 * j + 4)
                dve.wait_ge(m_Y, 4 * j + 4)
                dve.tensor_tensor(resid[:, ts, :], bank(j).rearrange("p (t d) -> p t d", t=4),
                                  x_tok[:, ts, :], ALU.add).then_inc(m_res, 1)
                dve.wait_ge(m_res, j + 1)
                ln_statistics(dve, CT + 4 * j, resid[:, ts, :], 4, 4 * j)
            for j in range(2):
                ts = slice(4 * j, 4 * j + 4)
                ln_apply(dve, CT + 4 * j, resid[:, ts, :], x1[:, ts, :], 4, 4 * j)
                dve.wait_ge(ln_out, CT + 4 * j + 4)
                ln_statistics(dve, CT + 8 + 4 * j, x1[:, ts, :], 4, 4 * j)
            for j in range(2):
                ts = slice(4 * j, 4 * j + 4)
                ln_apply(dve, CT + 8 + 4 * j, x1[:, ts, :], lat[:, ts, :], 4, 4 * j)
            nt_split(dve, 0, CT, cT_hi, cT_lo)
            nt_split(dve, CT, NT, xT_hi, xT_lo)

        @block.scalar
        def _(act):
            nt_scalar(act, 0, CT, 4, V_CTX)
            for j in range(2):
                act.wait_ge(nt_lo, CT)
                nt_scalar(act, CT + 4 * j, 4, 2 + j, V_LAT, j)

        @block.gpsimd
        def _(pool):
            def low_parts(heads):
                for h in heads:
                    pool.wait_ge(p_xwhi, h + 1)
                    pool.tensor_tensor(xw_lo[:, h, :], xw_raw[:, h, :],
                                       xw_hi[:, h, :].bitcast(F32), ALU.subtract).then_inc(p_xwlo, 1)
            ln_gpsimd(pool, 0, CT)
            low_parts(range(0, 4))
            ln_gpsimd(pool, CT, 4)
            ln_gpsimd(pool, CT + 4, 4, 4)
            ln_gpsimd(pool, CT + 8, 4)
            ln_gpsimd(pool, CT + 12, 4, 4)
            low_parts(range(4, HP))

        @block.sync
        def _(sp):
            sp.dma_start(xw_raw[:], a["x_w"]).then_inc(in_xw, 16)
            sp.wait_ge(m_Y, NT)
            sp.dma_start(wo[:], a["x_wo"]).then_inc(in_fw, 16)

    with ExitStack() as stage:
        wq_hi = sb("wq_hi", [P, 2, P], F32R, stage)
        wq_lo = sb("wq_lo", [P, 2, P], F32R, stage)
        krot = sb("krot", [P, 2, 3, 512], F32, stage)
        kS = sb("kS", [P, 2, 2, SC], F32R, stage)
        qS = sb("qS", [P, 2, 2, 2, S], F32R, stage)
        xv = sb("xv", [P, 4, 4, 2, XD + 1], F32, stage)
        xp = sb("xp", [P, 2, 2, 4, S], F32, stage)
        xrd = sb("xrd", [P, 2, 2, 2], F32, stage)
        xo = sb("xo", [P, 2, 2, 2, XD], F32, stage)
        KV, TB, QB, SB = 0, 2, 3, 4
        kv = PS[:, KV:KV + 2, :].rearrange("p a (s n) -> p (a s) n", n=256)
        N = 4 * HP
        x_ones, x_wq, x_K, x_t1, x_t2, x_sum, x_T, x_khi, x_klo, x_Q, x_qhi, x_qlo = (
            sem(n) for n in ("x_ones", "x_wq", "x_K", "x_t1", "x_t2", "x_sum", "x_T", "x_khi",
                             "x_klo", "x_Q", "x_qhi", "x_qlo"))
        x_S, x_exp, x_clip, x_vsb, x_O, x_rd, x_on, x_OT, x_out = (
            sem(n) for n in ("x_S", "x_exp", "x_clip", "x_vsb", "x_O", "x_rd", "x_on",
                             "x_OT", "x_out"))

        with nc.Block() as block:
            @block.tensor
            def _(pe):
                def step(h, c):
                    hh, b, u = at(h, c, 0)
                    if live(u, N):
                        wait(pe, x_vsb, u)
                        for st in range(4):
                            t = slice((4 * b + st) * P, (4 * b + st + 1) * P)
                            last = mm3(pe, kv[:, st, :], cT_hi[:, t], cT_lo[:, t],
                                       xw_hi[:, hh, 256:512], xw_lo[:, hh, 256:512])
                        last.then_inc(x_K, 1)
                    hh, b, u = at(h, c, 1)
                    if live(u, N):
                        wait(pe, x_wq, 2 * hh + 2)
                        wait(pe, x_qlo, u)
                        wait(pe, x_on, u - 2)
                        t = slice(b * S, (b + 1) * S)
                        for i in range(2):
                            last = mm3(pe, PS[:, QB, i * S:(i + 1) * S], wq_hi[:, i, :],
                                       wq_lo[:, i, :], xT_hi[:, t], xT_lo[:, t])
                        last.then_inc(x_Q, 1)
                        wait(pe, x_sum, 2 * u + 2)
                        wait(pe, x_out, u - 3)
                        wait(pe, x_klo, 2 * u)
                        for st in range(4):
                            last = pe.transpose(PS[:, TB, st * P:(st + 1) * P],
                                                krot[:, b % 2, 2, st * P:(st + 1) * P], ident)
                        last.then_inc(x_T, 1)
                    hh, b, u = at(h, c, 2)
                    if live(u, N):
                        for i in range(2):
                            wait(pe, x_klo, 2 * u + i + 1)
                            if i == 0:
                                wait(pe, x_qlo, u + 1)
                            wait(pe, x_exp, 2 * u + i - 1)
                            for st in range(4):
                                o = PS[:, SB + 2 * i + st // 2, (st % 2) * S:(st % 2 + 1) * S]
                                k = kS[:, b % 2, i, st * P:(st + 1) * P]
                                pe.matmul(o, k, qS[:, b % 2, 0, i, :], start=True, stop=False)
                                last = pe.matmul(o, k, qS[:, b % 2, 1, i, :], start=False, stop=True)
                            last.then_inc(x_S, 1)
                    hh, b, u = at(h, c, 3)
                    if live(u, N):
                        wait(pe, x_clip, 2 * u + 2)
                        wait(pe, x_on, u)
                        wait(pe, x_vsb, u + 1)
                        wait(pe, x_qlo, capped(u + 3, N))
                        for i in range(2):
                            for nt in range(2):
                                for st in range(4):
                                    last = pe.matmul(
                                        PS[:, QB, (2 * nt + i) * (XD + 1):(2 * nt + i + 1) * (XD + 1)],
                                        xp[:, b % 2, i, st, nt * P:(nt + 1) * P],
                                        xv[:, b, st, i, :], start=(st == 0), stop=(st == 3))
                        last.then_inc(x_O, 1)
                    hh, b, u = at(h, c, 4)
                    if live(u, N):
                        wait(pe, x_on, u + 1)
                        wait(pe, x_out, u)
                        wait(pe, x_klo, capped(2 * u + 8, 2 * N))
                        for nt in range(2):
                            last = pe.transpose(PS[:, TB, nt * P:(nt + 1) * P],
                                                xo[:, b % 2, nt, :, :], ident)
                        last.then_inc(x_OT, 1)
                pe.wait_ge(x_ones, 1)
                pipeline(pe, HP, step, 4)

            @block.scalar
            def _(act):
                def step(h, c):
                    hh, b, u = at(h, c, 1)
                    if live(u, N):
                        wait(act, x_S, 2 * u - 2)
                        act.wait_ge(x_Q, u + 1)
                        act.copy(qS[:, b % 2, 0, :, :].rearrange("p i n -> p (i n)"), bank(QB))\
                           .then_inc(x_qhi, 1)
                        act.wait_ge(x_T, u + 1)
                        act.copy(kS[0:64, b % 2, 0, :], PS[0:64, TB, :]).then_inc(x_khi, 1)
                        act.copy(kS[64:128, b % 2, 1, :], PS[64:128, TB, :]).then_inc(x_khi, 1)
                    hh, b, u = at(h, c, 0)
                    if live(u, N):
                        act.wait_ge(x_t2, u + 1)
                        wait(act, x_O, u - 3)
                        act.copy(xv[:, b, :, :, 0:XD],
                                 kv[:, :, P:2 * P].rearrange("p s (i d) -> p s i d", i=2)).then_inc(x_vsb, 1)
                    hh, b, u = at(h, c, 2)
                    if live(u, N):
                        wait(act, x_O, u - 1)
                        for i in range(2):
                            act.wait_ge(x_S, 2 * u + i + 1)
                            act.activation(xp[:, b % 2, i, :, :].rearrange("p s n -> p (s n)"),
                                           PS[:, SB + 2 * i:SB + 2 * i + 2, :].rearrange("p a n -> p (a n)"),
                                           ACT.Exp, scale=XD ** -0.5).then_inc(x_exp, 1)
                    hh, b, u = at(h, c, 4)
                    if live(u, N):
                        act.wait_ge(x_OT, u + 1)
                        act.wait_ge(in_const, 32)
                        act.copy(OT[:, hh, b * S:(b + 1) * S], PS[:, TB, 0:S]).then_inc(x_out, 1)
                pipeline(act, HP, step, 4)

            @block.vector
            def _(dve):
                dve.memset(xv[:, :, :, :, XD:XD + 1], 1.0).then_inc(x_ones, 1)

                def step(h, c):
                    hh, b, u = at(h, c, 4)
                    if live(u, N):
                        dve.wait_ge(x_O, u + 1)
                        o = PS[:, QB, 0:4 * (XD + 1)].rearrange("p (g d) -> p g d", g=4)
                        dve.reciprocal(xrd[:, b % 2, :, :].rearrange("p a b -> p (a b)"), o[:, :, XD])\
                           .then_inc(x_rd, 1)
                        dve.wait_ge(x_rd, u + 1)
                        wait(dve, x_OT, u - 1)
                        dve.tensor_tensor(
                            xo[:, b % 2, :, :, :].rearrange("p a b d -> p (a b) d"), o[:, :, 0:XD],
                            xrd[:, b % 2, :, :].rearrange("p a b -> p (a b)").unsqueeze(2)
                            .to_broadcast([P, 4, XD]), ALU.mult).then_inc(x_on, 1)
                    hh, b, u = at(h, c, 0)
                    if live(u, N):
                        wait(dve, x_sum, 2 * u - 2)
                        dve.wait_ge(x_K, u + 1)
                        k = kv[:, :, 0:P]
                        dve.tensor_tensor(krot[:, b % 2, 0, :].rearrange("p (s n) -> p s n", s=4), k,
                                          x_rope[:, 0, :].rearrange("p (s n) -> p s n", s=4), ALU.mult)\
                           .then_inc(x_t1, 1)
                        halves = "p (s a i) -> p s a i"
                        dve.tensor_tensor(krot[:, b % 2, 1, :].rearrange(halves, s=4, a=2),
                                          k.rearrange("p s (a i) -> p s a i", a=2)[:, :, ::-1, :],
                                          x_rope[:, 1, :].rearrange(halves, s=4, a=2), ALU.mult)\
                           .then_inc(x_t2, 1)
                    hh, b, u = at(h, c, 1)
                    if live(u, N):
                        dve.wait_ge(x_qhi, u + 1)
                        dve.tensor_tensor(qS[:, b % 2, 1, :, :].rearrange("p i n -> p (i n)"), bank(QB),
                                          qS[:, b % 2, 0, :, :].rearrange("p i n -> p (i n)").bitcast(F32),
                                          ALU.subtract).then_inc(x_qlo, 1)
                        dve.wait_ge(x_khi, 2 * u + 1)
                        dve.tensor_tensor(kS[64:128, b % 2, 0, :], PS[0:64, TB, :],
                                          kS[0:64, b % 2, 0, :].bitcast(F32), ALU.subtract)\
                           .then_inc(x_klo, 1)
                        dve.wait_ge(x_khi, 2 * u + 2)
                        dve.tensor_tensor(kS[0:64, b % 2, 1, :], PS[64:128, TB, :],
                                          kS[64:128, b % 2, 1, :].bitcast(F32), ALU.subtract)\
                           .then_inc(x_klo, 1)
                    hh, b, u = at(h, c, 2)
                    if live(u, N):
                        for i in range(2):
                            dve.wait_ge(x_exp, 2 * u + i + 1)
                            p = xp[:, b % 2, i, :, :].rearrange("p s n -> p (s n)")
                            dve.tensor_scalar(p, p, CLIP_LO, CLIP_HI, ALU.max, ALU.min)\
                               .then_inc(x_clip, 1)
                pipeline(dve, HP, step, 4)

            @block.gpsimd
            def _(pool):
                def stage_wq(hh, g):
                    wait(pool, x_Q, 4 * g)
                    pool.wait_ge(p_xwlo, HP)
                    for dst, src in ((wq_hi, xw_hi), (wq_lo, xw_lo)):
                        pool.tensor_copy(dst[:].rearrange("p i n -> p (i n)"),
                                         src[:, hh, 0:256].bitcast(F32)).then_inc(x_wq, 1)

                def step(h, c):
                    hh, b, u = at(h, c, 0)
                    if live(u, N):
                        if c == 0:
                            stage_wq(hh, hh)
                        wait(pool, x_T, u - 1)
                        pool.wait_ge(x_t2, u + 1)
                        for i in range(2):
                            t1, t2 = (krot[:, b % 2, j, :].rearrange("p (s a h i) -> p s a h i", s=4, a=2, h=2)
                                      [:, :, :, i, :] for j in range(2))
                            o = krot[:, b % 2, 2, :].rearrange("p (s h a i) -> p s h a i", s=4, a=2, h=2)
                            pool.tensor_tensor(o[:, :, i, :, :], t1, t2, ALU.add).then_inc(x_sum, 1)
                pipeline(pool, HP, step, 0)


    cross.close()
    experts = sb("experts", [P, E, N_EXP])
    gT = sb("gT", [2 * E, T], F32R)
    sel = sb("sel", [2 * E, E, P], F32R)
    accT = sb("accT", [P, T])
    gateb = OT

    m2_Y, m2_res, m2_bo = sem("m2_Y"), sem("m2_res"), sem("m2_bo")
    f_whi, f_wlo, f_P, f_F, f_r, f_G, f_st, f_Vp, f_v, f_vones = (sem(n) for n in (
        "f_whi", "f_wlo", "f_P", "f_F", "f_r", "f_G", "f_st", "f_Vp", "f_v", "f_vones"))
    with ExitStack() as stage:
        qk_st = sb("qk_st", [P, 2, NQ, T], F32R)
        fv = sb("fv", [P, NT, FH, 32], F32)
        fo = x1

        with ExitStack() as early:
            fw_hi = sb("fw_hi", [P, 2 * NQ * P], F32R, early)
            fw_lo = sb("fw_lo", [P, 2 * NQ * P], F32R, early)
            fv_hi = sb("fv_hi", [P, D], F32R, early)
            fv_lo = sb("fv_lo", [P, D], F32R, early)
            bv4 = sb("bv4", [P, 4 * FH, FD], F32, early)
            pf = [featT[:, T:T + 512], featT[:, T + 512:2 * T],
                  x_tok[:, 0:4, :].rearrange("p t d -> p (t d)"), x_tok[:, 4:8, :].rearrange("p t d -> p (t d)")]
            pr = sb("pr", [P, 2, 512], F32R, early)
            pg = norm[:, NT:2 * NT, :].rearrange("p (a t) d -> p a (t d)", a=2)
            with nc.Block() as block:
                @block.tensor
                def _(pe):
                    pe.wait_ge(in_fw, 112)
                    for t in range(NT):
                        for h in range(HP):
                            last = pe.matmul(PS[:, t // 4, (t % 4) * P:(t % 4 + 1) * P],
                                             OT[:, h, t * P:(t + 1) * P], wo[:, h, :],
                                             start=(h == 0), stop=(h == HP - 1))
                        last.then_inc(m2_Y, 1)
                    nt_tensor(pe, CT + 3 * NT, norm[:, 0:4, :], 4, 2)
                    nt_tensor(pe, CT + 3 * NT + 4, norm[:, 4:8, :], 4, 3)
                    pe.wait_ge(f_wlo, 2)
                    for g in range(4 * NQ):
                        n, w = g // (2 * NQ), g % (2 * NQ)
                        pe.wait_ge(nt_lo, CT + NT + 4 * n + 4)
                        wait(pe, f_r, g - 3)
                        c = slice(n * 512, (n + 1) * 512)
                        mm3(pe, bank(4 + g % 4), fw_hi[:, w * P:(w + 1) * P], fw_lo[:, w * P:(w + 1) * P],
                            xT_hi[:, c], xT_lo[:, c]).then_inc(f_P, 1)
                    for t in range(NT):
                        c = slice(t * P, (t + 1) * P)
                        mm3(pe, PS[:, t // 4, (t % 4) * P:(t % 4 + 1) * P], xT_hi[:, c], xT_lo[:, c],
                            fv_hi[:], fv_lo[:]).then_inc(f_Vp, 1)

                @block.vector
                def _(dve):
                    for j in range(2):
                        ts = slice(4 * j, 4 * j + 4)
                        dve.wait_ge(m2_Y, 4 * j + 4)
                        dve.tensor_tensor(resid[:, ts, :], bank(j).rearrange("p (t d) -> p t d", t=4),
                                          x1[:, ts, :], ALU.add).then_inc(m2_res, 1)
                        dve.wait_ge(m2_res, j + 1)
                        dve.tensor_tensor(resid[:, ts, :], resid[:, ts, :],
                                          rows[:, 0:1, :].to_broadcast([P, 4, D]), ALU.add)\
                           .then_inc(m2_bo, 1)
                        dve.wait_ge(m2_bo, j + 1)
                        ln_statistics(dve, CT + 2 * NT + 4 * j, resid[:, ts, :], 4, 4 * j)
                    for j in range(2):
                        ts, n_ln = slice(4 * j, 4 * j + 4), CT + 2 * NT + 4 * j
                        ln_apply(dve, n_ln, resid[:, ts, :], x2[:, ts, :], 4, 4 * j)
                        dve.wait_ge(ln_out, n_ln + 4)
                        ln_statistics(dve, n_ln + 8, x2[:, ts, :], 4, 4 * j)
                    for j in range(2):
                        ts = slice(4 * j, 4 * j + 4)
                        ln_apply(dve, CT + 3 * NT + 4 * j, x2[:, ts, :], norm[:, ts, :], 4, 4 * j)
                    nt_split(dve, CT + NT, NT, xT_hi, xT_lo)
                    for k in range(4 * NQ + 1):
                        g = k
                        ab = C_AB + 2 * (g % (2 * NQ) // NQ)
                        if 0 <= g < 4 * NQ:
                            wait(dve, f_st, g - 1)
                            dve.wait_ge(f_r, g + 1)
                            dve.tensor_scalar(pg[:, g % 2, :], pr[:, g % 2, :].bitcast(F32),
                                              const[:, ab + 1:ab + 2], None, ALU.mult).then_inc(f_G, 1)
                        g = k - 1
                        n, w = g // (2 * NQ), g % (2 * NQ)
                        ab = C_AB + 2 * (w // NQ)
                        if 0 <= g < 4 * NQ:
                            dve.wait_ge(f_F, g + 1)
                            dve.wait_ge(f_G, g + 1)
                            dve.scalar_tensor_tensor(qk_st[:, w // NQ, w % NQ, n * 512:(n + 1) * 512],
                                                     pf[g % 4], const[:, ab:ab + 1], pg[:, g % 2, :],
                                                     ALU.mult, ALU.add).then_inc(f_st, 1)
                    for j in range(2):
                        dve.wait_ge(f_Vp, 4 * j + 4)
                        dve.tensor_tensor(
                            fv[:, 4 * j:4 * j + 4, :, 0:FD].rearrange("p t h d -> p (t h) d"),
                            bank(j).rearrange("p (t d) -> p t d", d=FD),
                            bv4[:], ALU.add).then_inc(f_v, 1)

                @block.scalar
                def _(act):
                    nt_scalar(act, CT + NT, NT, 2, V_LN1)
                    for g in range(4 * NQ):
                        w = g % (2 * NQ)
                        act.wait_ge(f_P, g + 1)
                        wait(act, f_st, g - 3)
                        act.activation(pf[g % 4], bank(4 + g % 4), ACT.Identity,
                                       bias=vec[:, V_BQK + w:V_BQK + w + 1]).then_inc(f_F, 1)
                        wait(act, f_G, g - 1)
                        act.activation(pr[:, g % 2, :], bank(4 + g % 4), ACT.Identity,
                                       bias=vec[:, V_BQK + w:V_BQK + w + 1]).then_inc(f_r, 1)

                @block.sync
                def _(sp):
                    for e in range(E):
                        sp.dma_start(experts[:, e, :], a["experts"][e]).then_inc(in_ex, 16)

                @block.gpsimd
                def _(pool):
                    pool.tensor_copy(fw_hi[:], f_wqk[:]).then_inc(f_whi, 1)
                    pool.tensor_copy(fv_hi[:], f_wvo[:, 0, :]).then_inc(f_whi, 1)
                    for t in range(4):
                        pool.tensor_copy(bv4[:, 16 * t:16 * t + 16, :],
                                         rows[:, 2, :].rearrange("p (h d) -> p h d", d=FD)).then_inc(f_whi, 1)
                    pool.wait_ge(f_whi, 6)
                    pool.tensor_tensor(fw_lo[:], f_wqk[:], fw_hi[:].bitcast(F32), ALU.subtract)\
                        .then_inc(f_wlo, 1)
                    pool.tensor_tensor(fv_lo[:], f_wvo[:, 0, :], fv_hi[:].bitcast(F32), ALU.subtract)\
                        .then_inc(f_wlo, 1)
                    pool.memset(fv[:, :, :, FD:], 0.0).then_inc(f_vones, 1)
                    pool.wait_ge(f_vones, 1)
                    pool.memset(fv[:, :, :, FD:FD + 1], 1.0).then_inc(f_vones, 1)
                    for j in range(4):
                        ln_gpsimd(pool, CT + 2 * NT + 4 * j, 4, 4 * (j % 2))

        PT, OB = 4, 7
        N = 4 * NQ
        attn = ExitStack()
        fs = sb("fs", [P, 2, 4, 3 * P], F32, attn)
        fmx = sb("fmx", [P, 2, 2, 4], F32, attn)
        fpT = sb("fpT", [P, 2, 12, P], F32, attn)
        frd = sb("frd", [P, 2, 8], F32, attn)
        foT = featT[:, 0:2 * S].rearrange("p (a n) -> p a n", a=2)
        c_S, c_max, c_sub, c_exp, c_PT, c_pT, c_O, c_oT, c_OT, c_rd, c_on = (sem(n) for n in (
            "c_S", "c_max", "c_sub", "c_exp", "c_PT", "c_pT", "c_O", "c_oT", "c_OT", "c_rd", "c_on"))
        with nc.Block() as block:
            @block.tensor
            def _(pe):
                for k in range(N + 3):
                    u = k - 3
                    if 0 <= u < N:
                        pe.wait_ge(c_oT, u + 1)
                        for it in range(2):
                            last = pe.transpose(PS[:, OB, it * P:(it + 1) * P],
                                                foT[:, u % 2, it * P:(it + 1) * P], ident)
                        last.then_inc(c_OT, 1)
                    u = k
                    if u < N:
                        q, b = u // 4, u % 4
                        for pair in (0,):
                            wait(pe, c_sub, 4 * (u - 1) + 2 * pair + 2)
                            for hh in (2 * pair, 2 * pair + 1):
                                pe.matmul(PS[:, hh, 0:384], ident16[:], mask16[:], start=True,
                                          stop=False, skip_group_check=True)
                            for hh in (2 * pair, 2 * pair + 1):
                                r = slice(32 * hh, 32 * hh + 32)
                                qs, ks = qk_st[r, 0, q, :], qk_st[r, 1, q, :]
                                pe.matmul(PS[:, hh, 0:P], qs[:, b * S:b * S + P], ks[:, b * S:b * S + P],
                                          start=False, stop=False, skip_group_check=True)
                                last = pe.matmul(PS[:, hh, P:384], qs[:, b * S + P:b * S + 2 * P],
                                                 ks[:, b * S:(b + 1) * S], start=False, stop=True,
                                                 skip_group_check=True)
                            last.then_inc(c_S, 1)
                    u = k
                    if u < N:
                        q, b = u // 4, u % 4
                        for pair in (1,):
                            wait(pe, c_sub, 4 * (u - 1) + 2 * pair + 2)
                            for hh in (2 * pair, 2 * pair + 1):
                                pe.matmul(PS[:, hh, 0:384], ident16[:], mask16[:], start=True,
                                          stop=False, skip_group_check=True)
                            for hh in (2 * pair, 2 * pair + 1):
                                r = slice(32 * hh, 32 * hh + 32)
                                qs, ks = qk_st[r, 0, q, :], qk_st[r, 1, q, :]
                                pe.matmul(PS[:, hh, 0:P], qs[:, b * S:b * S + P], ks[:, b * S:b * S + P],
                                          start=False, stop=False, skip_group_check=True)
                                last = pe.matmul(PS[:, hh, P:384], qs[:, b * S + P:b * S + 2 * P],
                                                 ks[:, b * S:(b + 1) * S], start=False, stop=True,
                                                 skip_group_check=True)
                            last.then_inc(c_S, 1)
                    u = k - 2
                    if 0 <= u < N:
                        q, b = u // 4, u % 4
                        pe.wait_ge(c_pT, u + 1)
                        wait(pe, c_on, u)
                        for hh in range(4):
                            v = fv[:, 2 * b:2 * b + 2, 4 * q + hh, :]
                            o = PS[32 * hh:32 * hh + 32, OB, 0:S]
                            pe.matmul(o, v[:, 0, :], fpT[:, u % 2, 3 * hh:3 * hh + 2, :],
                                      start=True, stop=False, skip_group_check=True)
                            last = pe.matmul(o[:, P:S], v[:, 1, :], fpT[:, u % 2, 3 * hh + 2, :],
                                             start=False, stop=True, skip_group_check=True)
                        last.then_inc(c_O, 1)
                    u = k - 1
                    if 0 <= u < N:
                        pe.wait_ge(c_exp, u + 1)
                        wait(pe, c_pT, u)
                        for j in range(12):
                            last = pe.transpose(PS[:, PT + j // 4, (j % 4) * P:(j % 4 + 1) * P],
                                                fs[:, u % 2, j // 3, (j % 3) * P:(j % 3 + 1) * P], ident)
                        last.then_inc(c_PT, 1)

            @block.vector
            def _(dve):
                for k in range(N + 3):
                    u = k - 3
                    if 0 <= u < N:
                        q, b = u // 4, u % 4
                        dve.wait_ge(c_OT, u + 1)
                        o = PS[:, OB, 0:S].rearrange("p (g d) -> p g d", d=32)
                        dve.reciprocal(frd[:, u % 2, :], o[:, :, FD]).then_inc(c_rd, 1)
                        dve.wait_ge(c_rd, u + 1)
                        dve.tensor_tensor(
                            fo[:, 2 * b:2 * b + 2, 32 * q:32 * q + 32].rearrange("p t (h d) -> p t h d", d=FD),
                            o[:, :, 0:FD].rearrange("p (t h) d -> p t h d", t=2),
                            frd[:, u % 2, :].rearrange("p (t h) -> p t h", t=2).unsqueeze(3)
                            .to_broadcast([P, 2, 4, FD]), ALU.mult).then_inc(c_on, 1)
                    u = k
                    if u < N:
                        for pair in range(2):
                            hs = slice(2 * pair, 2 * pair + 2)
                            dve.wait_ge(c_S, 2 * u + pair + 1)
                            for it in range(2):
                                cols = slice(P * it, P + 256 * it)
                                dve.tensor_reduce(fmx[:, u % 2, it, hs], PS[:, hs, cols], AX.X, ALU.max)\
                                   .then_inc(c_max, 1)
                            wait(dve, c_PT, u - 1)
                            for it in range(2):
                                cols = slice(P * it, P + 256 * it)
                                dve.wait_ge(c_max, 4 * u + 2 * pair + it + 1)
                                dve.tensor_tensor(
                                    fs[:, u % 2, hs, cols], PS[:, hs, cols],
                                    fmx[:, u % 2, it, hs].unsqueeze(2).to_broadcast([P, 2, P + P * it]),
                                    ALU.subtract).then_inc(c_sub, 1)

            @block.scalar
            def _(act):
                for k in range(N + 2):
                    u = k - 2
                    if 0 <= u < N:
                        act.wait_ge(c_O, u + 1)
                        wait(act, c_OT, u - 1)
                        act.copy(foT[:, u % 2, :], PS[:, OB, 0:S]).then_inc(c_oT, 1)
                    u = k - 1
                    if 0 <= u < N:
                        act.wait_ge(c_PT, u + 1)
                        wait(act, c_O, u - 1)
                        act.copy(fpT[:, u % 2, :, :].rearrange("p a b -> p (a b)"),
                                 PS[:, PT:PT + 3, :].rearrange("p a b -> p (a b)")).then_inc(c_pT, 1)
                    u = k
                    if u < N:
                        act.wait_ge(c_sub, 4 * u + 4)
                        e = fs[:, u % 2, :, :].rearrange("p a b -> p (a b)")
                        act.activation(e, e, ACT.Exp, scale=FD ** -0.5).then_inc(c_exp, 1)

        attn.close()

        w_hi = sb("w_hi", [P, 2, 2 * FF], F32R)
        w_lo = sb("w_lo", [P, 2, 2 * FF], F32R)
        b1 = sb("b1", [P, 2, FT], F32)
        e_whi, e_wlo, e_b1 = sem("e_whi"), sem("e_wlo"), sem("e_b1")
        with ExitStack() as early:
            oT = featT[:, T:2 * T]
            x3 = norm[:, NT:2 * NT, :]
            gl = sb("gl", [P, NT, E], F32, early)
            top = sb("top", [P, NT, 8], F32, early)
            topi = sb("topi", [P, NT, 8], U32, early)
            topf = sb("topf", [P, NT, 2], F32, early)
            gw = sb("gw", [P, 4, NT], F32, early)
            g1 = sb("g1", [P, NT, E], F32, early)
            g2 = sb("g2", [P, NT, E], F32, early)
            gates = sb("gates", [P, NT, E], F32, early)
            ghi = sb("ghi", [P, NT, E], F32R, early)
            gparts = sb("gparts", [P, NT, 2, E], F32, early)
            d_T, d_foT, d_Y, d_r1, d_x3, d_r2, d_G, d_gl, d_top, d_ti, d_tf, d_w, d_e, d_gs = (
                sem(n) for n in ("d_T", "d_foT", "d_Y", "d_r1", "d_x3", "d_r2", "d_G", "d_gl",
                                 "d_top", "d_ti", "d_tf", "d_w", "d_e", "d_gs"))
            d_hi, d_parts, d_gT, d_gTs, d_B, d_acc, d_bc, d_Gs, d_sel = (sem(n) for n in (
                "d_hi", "d_parts", "d_gT", "d_gTs", "d_B", "d_acc", "d_bc", "d_Gs", "d_sel"))
            with nc.Block() as block:
                @block.tensor
                def _(pe):
                    for t in range(NT):
                        pe.transpose(PS[:, t // 4, (t % 4) * P:(t % 4 + 1) * P], fo[:, t, :], ident)\
                          .then_inc(d_T, 1)
                    for t in range(NT):
                        pe.wait_ge(d_foT, t // 4 + 1)
                        pe.matmul(PS[:, 2 + t // 4, (t % 4) * P:(t % 4 + 1) * P],
                                  oT[:, t * P:(t + 1) * P], f_wvo[:, 1, :], start=True, stop=True)\
                          .then_inc(d_Y, 1)
                    nt_tensor(pe, CT + 4 * NT, norm, NT, 4)
                    for t in range(NT):
                        pe.wait_ge(nt_act, CT + 2 * NT + 4 * (t // 4) + 4)
                        pe.matmul(PS[:, 6, t * E:(t + 1) * E], featT[:, t * P:(t + 1) * P], gate_w[:],
                                  start=True, stop=True).then_inc(d_G, 1)
                    pe.wait_ge(d_parts, 2)
                    for t in range(NT):
                        pe.transpose(PS[0:2 * E, t // 4, (t % 4) * P:(t % 4 + 1) * P],
                                     gparts[:, t, :, :], ident).then_inc(d_gT, 1)
                    for n in range(2):
                        pe.wait_ge(d_gTs, n + 1)
                        pe.matmul(bank(2 + n), fc2_b[:], gT[:, n * 512:(n + 1) * 512].bitcast(F32),
                                  start=True, stop=True).then_inc(d_B, 1)

                @block.scalar
                def _(act):
                    for j in range(2):
                        act.wait_ge(d_T, 4 * j + 4)
                        act.copy(oT[:, j * 512:(j + 1) * 512], bank(j)).then_inc(d_foT, 1)
                    act.wait_ge(in_ex, 16 * E)
                    act.copy(w_hi[:, 0, :], experts[:, 0, 0:2 * FF]).then_inc(e_whi, 1)
                    nt_scalar(act, CT + 2 * NT, NT, 4, V_LN2)
                    act.wait_ge(d_w, 1)
                    act.activation(gw[:, 1, :], gw[:, 0, :], ACT.Exp).then_inc(d_e, 1)
                    for j in range(2):
                        act.wait_ge(d_gT, 4 * j + 4)
                        act.copy(gT[:, j * 512:(j + 1) * 512], PS[0:2 * E, j, :]).then_inc(d_gTs, 1)
                    for n in range(2):
                        act.wait_ge(d_B, n + 1)
                        act.copy(accT[:, n * 512:(n + 1) * 512], bank(2 + n)).then_inc(d_acc, 1)

                @block.gpsimd
                def _(pool):
                    pool.tensor_copy(sel[:].rearrange("p e m -> p (e m)"), const[0:2 * E, C_SEL:C_SEL + E * P])\
                        .then_inc(d_sel, 1)
                    for j in range(2):
                        ln_gpsimd(pool, CT + 4 * NT + 4 * j, 4, 4 * j)
                    pool.wait_ge(e_whi, 1)
                    pool.tensor_tensor(w_lo[:, 0, :], experts[:, 0, 0:2 * FF], w_hi[:, 0, :].bitcast(F32),
                                       ALU.subtract).then_inc(e_wlo, 1)
                    pool.tensor_copy(b1[:, 0, :], experts[:, 0, WB:WB + FT]).then_inc(e_b1, 1)
                    pool.wait_ge(d_x3, 2)
                    pool.tensor_tensor(resid[:], x2[:], x3, ALU.add).then_inc(d_r2, 1)

                @block.vector
                def _(dve):
                    for j in range(2):
                        ts = slice(4 * j, 4 * j + 4)
                        dve.wait_ge(d_Y, 4 * j + 4)
                        dve.tensor_tensor(x3[:, ts, :], bank(2 + j).rearrange("p (t d) -> p t d", t=4),
                                          x2[:, ts, :], ALU.add).then_inc(d_r1, 1)
                        dve.wait_ge(d_r1, j + 1)
                        dve.tensor_tensor(x3[:, ts, :], x3[:, ts, :],
                                          rows[:, 1:2, :].to_broadcast([P, 4, D]), ALU.add)\
                           .then_inc(d_x3, 1)
                        dve.wait_ge(d_x3, j + 1)
                        ln_statistics(dve, CT + 4 * NT + 4 * j, x3[:, ts, :], 4, 4 * j)
                    for j in range(2):
                        ts = slice(4 * j, 4 * j + 4)
                        ln_apply(dve, CT + 4 * NT + 4 * j, x3[:, ts, :], norm[:, ts, :], 4, 4 * j)
                    nt_split(dve, CT + 2 * NT, NT, xT_hi, xT_lo)
                    dve.wait_ge(d_G, NT)
                    dve.tensor_copy(gl[:].rearrange("p t e -> p (t e)"), PS[:, 6, 0:NT * E]).then_inc(d_gl, 1)
                    dve.wait_ge(d_gl, 1)
                    for t in range(NT):
                        dve.max(out=top[:, t, :], in_=gl[:, t, :]).then_inc(d_top, 1)
                    for t in range(NT):
                        dve.wait_ge(d_top, t + 1)
                        dve.max_index(out=topi[:, t, :], in_max=top[:, t, :], in_values=gl[:, t, :])\
                           .then_inc(d_ti, 1)
                    dve.tensor_tensor(gw[:, 0, :], top[:, :, 1], top[:, :, 0], ALU.subtract).then_inc(d_w, 1)
                    dve.wait_ge(d_ti, NT)
                    dve.tensor_copy(topf[:], topi[:, :, 0:2]).then_inc(d_tf, 1)
                    dve.wait_ge(d_tf, 1)
                    for i, g in enumerate((g1, g2)):
                        dve.tensor_tensor(g[:], const[:, C_IOTA:C_IOTA + E].unsqueeze(1).to_broadcast([P, NT, E]),
                                          topf[:, :, i:i + 1].to_broadcast([P, NT, E]), ALU.is_equal)\
                           .then_inc(d_gs, 1)
                    dve.wait_ge(d_e, 1)
                    dve.tensor_scalar(gw[:, 3, :], gw[:, 1, :], 1.0, None, ALU.add).then_inc(d_w, 1)
                    dve.wait_ge(d_w, 2)
                    dve.reciprocal(gw[:, 2, :], gw[:, 3, :]).then_inc(d_w, 1)
                    dve.wait_ge(d_w, 3)
                    dve.tensor_tensor(gw[:, 3, :], gw[:, 1, :], gw[:, 2, :], ALU.mult).then_inc(d_w, 1)
                    dve.wait_ge(d_w, 4)
                    dve.wait_ge(d_gs, 2)
                    for i, g in enumerate((g1, g2)):
                        dve.tensor_tensor(g[:], g[:], gw[:, 2 + i, :].unsqueeze(2).to_broadcast([P, NT, E]),
                                          ALU.mult).then_inc(d_gs, 1)
                    dve.wait_ge(d_gs, 4)
                    dve.tensor_tensor(gates[:], g1[:], g2[:], ALU.add).then_inc(d_gs, 1)
                    dve.wait_ge(d_gs, 5)
                    dve.tensor_copy(ghi[:], gates[:]).then_inc(d_hi, 1)
                    dve.wait_ge(d_hi, 1)
                    dve.tensor_copy(gparts[:, :, 0, :], ghi[:].bitcast(F32)).then_inc(d_parts, 1)
                    dve.tensor_tensor(gparts[:, :, 1, :], gates[:], ghi[:].bitcast(F32), ALU.subtract)\
                       .then_inc(d_parts, 1)

    with ExitStack() as stage:
        hf = fv[:, 0:4, :, :].rearrange("p t h d -> p (t h d)").rearrange("p (f n) -> p f n", f=4)
        h_hi, h_lo = (qk_st[:, j, 0:2, :].rearrange("p w n -> p (w n)").rearrange("p (f n) -> p f n", f=4)
                      for j in range(2))
        yg = sb("yg", [P, 2, 512], F32, stage)
        outt = sb("outt", [P, NT, D], F32, stage)
        e_H, e_gelu, e_hi, e_lo, e_Y, e_yg, e_acc = (
            sem(n) for n in ("e_H", "e_gelu", "e_hi", "e_lo", "e_Y", "e_yg", "e_acc"))
        HB, YB, GB = 0, 4, 6
        NG = 8 * E

        def experts_loop(eng, step):
            for s in range(16):
                step(0, s)
            with eng.Fori(1, E // 2 - 1) as i:
                for s in range(16):
                    step(i, s)
            for s in range(18):
                step(E // 2 - 1, s)

        with nc.Block() as block:
            @block.tensor
            def _(pe):
                def step(i, s):
                    if s < 16:
                        g, p, n, ft = 16 * i + s, s // 8, s % 8 // 4, s % 4
                        if s % 8 == 0:
                            pe.wait_ge(e_wlo, 2 * i + p + 1)
                        wait(pe, e_gelu, g - 3)
                        c = slice(n * 512, (n + 1) * 512)
                        w = slice(ft * P, (ft + 1) * P)
                        mm3(pe, bank(HB + ft), w_hi[:, p, w], w_lo[:, p, w], xT_hi[:, c], xT_lo[:, c])\
                            .then_inc(e_H, 1)
                        if isinstance(i, int) and i == 0:
                            wait(pe, d_Gs, s - 1)
                            pe.matmul(bank(GB + s % 2), sel[:, s // 2, :],
                                      gT[:, (s % 2) * 512:(s % 2 + 1) * 512], start=True, stop=True)\
                              .then_inc(d_bc, 1)
                    if s < 2 and isinstance(i, int) and i == 0:
                        return
                    g, r = 16 * i + s - 2, (s - 2) % 16
                    p, n, ft = r // 8, r % 8 // 4, r % 4
                    wait(pe, e_lo, g + 1)
                    if ft == 0:
                        wait(pe, e_yg, 4 * i + (s - 2) // 4 - 1)
                    w = slice(FF + ft * P, FF + (ft + 1) * P)
                    mm3(pe, bank(YB + n), w_hi[:, p, w], w_lo[:, p, w], h_hi[:, ft, :], h_lo[:, ft, :],
                        start=(ft == 0), stop=(ft == FT - 1)).then_inc(e_Y, 1)
                experts_loop(pe, step)

            @block.scalar
            def _(act):
                def step(i, s):
                    if s >= 16:
                        return
                    g, p, ft = 16 * i + s, s // 8, s % 4
                    wait(act, e_lo, g - 3)
                    if s % 8 == 0:
                        wait(act, e_b1, 2 * i + p + 1)
                    act.wait_ge(e_H, g + 1)
                    act.activation(hf[:, ft, :], bank(HB + ft), ACT.Gelu, bias=b1[:, p, ft:ft + 1])\
                       .then_inc(e_gelu, 1)
                    if isinstance(i, int) and i == 0:
                        act.wait_ge(d_bc, s + 1)
                        act.copy(gateb[:, s // 2, (s % 2) * 512:(s % 2 + 1) * 512], bank(GB + s % 2))\
                           .then_inc(d_Gs, 1)
                experts_loop(act, step)

            @block.vector
            def _(dve):
                def load(e, p):
                    wait(dve, e_Y, 8 * (e - 1))
                    wait(dve, e_wlo, e - 1)
                    dve.wait_ge(in_ex, 16 * E)
                    dve.tensor_copy(w_hi[:, p, :], experts[:, e, 0:2 * FF]).then_inc(e_whi, 1)
                    dve.tensor_copy(b1[:, p, :], experts[:, e, WB:WB + FT]).then_inc(e_b1, 1)

                def step(i, s):
                    if s % 8 == 2 and not (isinstance(i, int) and 2 * i + s // 8 + 1 >= E):
                        load(2 * i + s // 8 + 1, (s // 8 + 1) % 2)
                    if s < 17 and not (isinstance(i, int) and 16 * i + s < 1):
                        g, ft = 16 * i + s - 1, (s - 1) % 4
                        wait(dve, e_Y, g - 3)
                        dve.wait_ge(e_gelu, g + 1)
                        dve.tensor_copy(h_hi[:, ft, :], hf[:, ft, :]).then_inc(e_hi, 1)
                        dve.wait_ge(e_hi, g + 1)
                        dve.tensor_tensor(h_lo[:, ft, :], hf[:, ft, :], h_hi[:, ft, :].bitcast(F32),
                                          ALU.subtract).then_inc(e_lo, 1)
                    if (s - 2) % 4 == 3 and not (isinstance(i, int) and i == 0 and s < 2):
                        y, n = 4 * i + (s - 2) // 4, (s - 2) // 4 % 2
                        e = 2 * i + (s - 2) // 8
                        wait(dve, e_acc, y - 1)
                        dve.wait_ge(e_Y, 4 * y + 4)
                        dve.wait_ge(d_Gs, 4 * min(y, 3) + 4 if isinstance(y, int) else 16)
                        dve.tensor_tensor(yg[:, n, :], bank(YB + n),
                                          gateb[:, e, n * 512:(n + 1) * 512], ALU.mult).then_inc(e_yg, 1)
                experts_loop(dve, step)

            @block.gpsimd
            def _(pool):
                def load(e, p):
                    pool.wait_ge(e_whi, e + 1)
                    pool.wait_ge(in_ex, 16 * E)
                    pool.tensor_tensor(w_lo[:, p, :], experts[:, e, 0:2 * FF], w_hi[:, p, :].bitcast(F32),
                                       ALU.subtract).then_inc(e_wlo, 1)

                def step(i, s):
                    if s % 8 == 2 and not (isinstance(i, int) and 2 * i + s // 8 + 1 >= E):
                        load(2 * i + s // 8 + 1, (s // 8 + 1) % 2)
                    if (s - 2) % 4 == 3 and not (isinstance(i, int) and i == 0 and s < 2):
                        y, n = 4 * i + (s - 2) // 4, (s - 2) // 4 % 2
                        c = slice(n * 512, (n + 1) * 512)
                        wait(pool, e_acc, y - 1)
                        pool.wait_ge(e_yg, y + 1)
                        pool.tensor_tensor(accT[:, c], accT[:, c], yg[:, n, :], ALU.add).then_inc(e_acc, 1)
                experts_loop(pool, step)

        z_T, z_res, z_out = sem("z_T"), sem("z_res"), sem("z_out")
        with nc.Block() as block:
            @block.tensor
            def _(pe):
                for t in range(NT):
                    pe.transpose(PS[:, t // 4, (t % 4) * P:(t % 4 + 1) * P],
                                 accT[:, t * P:(t + 1) * P], ident).then_inc(z_T, 1)

            @block.vector
            def _(dve):
                for j in range(2):
                    ts = slice(4 * j, 4 * j + 4)
                    dve.wait_ge(z_T, 4 * j + 4)
                    dve.tensor_tensor(x1[:, ts, :], bank(j).rearrange("p (t d) -> p t d", t=4),
                                      resid[:, ts, :], ALU.add).then_inc(z_res, 1)
                    dve.wait_ge(z_res, j + 1)
                    ln_statistics(dve, CT + 5 * NT + 4 * j, x1[:, ts, :], 4, 4 * j)
                for j in range(2):
                    ts = slice(4 * j, 4 * j + 4)
                    ln_apply(dve, CT + 5 * NT + 4 * j, x1[:, ts, :], outt[:, ts, :], 4, 4 * j)

            @block.gpsimd
            def _(pool):
                for j in range(2):
                    ln_gpsimd(pool, CT + 5 * NT + 4 * j, 4, 4 * j)

            @block.sync
            def _(sp):
                for j in range(2):
                    sp.wait_ge(ln_out, CT + 5 * NT + 4 * j + 4)
                    sp.dma_start(out[:, 4 * j:4 * j + 4, :], outt[:, 4 * j:4 * j + 4, :]).then_inc(z_out, 16)
                sp.wait_ge(z_out, 32)


def constants():
    c = np.zeros((P, N_CONST), np.float32)
    c[:, C_ID:C_ID + P] = np.eye(P)
    c[:, C_MASK:C_MASK + P] = np.where(np.arange(P)[:, None] < np.arange(P)[None, :], MASKED, 0.0)
    c[:, C_IOTA:C_IOTA + E] = np.arange(E)
    part = np.arange(P) % 32 // FD
    q_low, k_low = part % 2, part // 2
    c[:, C_AB:C_AB + 4] = np.stack([q_low, 1 - 2 * q_low, k_low, 1 - 2 * k_low], 1)
    for e in range(E):
        c[[e, E + e], C_SEL + e * P:C_SEL + (e + 1) * P] = 1.0
    half = D // 2
    freq = np.power(np.float32(10000.0), -np.arange(half, dtype=np.float32) / np.float32(half))
    ang = np.arange(S, dtype=np.float32)[:, None] * freq.astype(np.float32)[None, :]
    cos, sin = np.cos(ang), np.sin(ang)
    cos = np.concatenate([cos, cos], 1).reshape(2, P, 1, D)
    sin = np.concatenate([-sin, sin], 1).reshape(2, P, 1, D)
    scale = np.array([1.0 / D, 1.0], np.float32)[None, None, :, None]
    rope = np.stack([np.broadcast_to(t * scale, (2, P, 2, D)) for t in (cos, sin)])
    rope = rope.transpose(2, 0, 1, 3, 4).reshape(P, 2, 512).astype(np.float32)
    return c, rope


def kernel(**x):
    import concourse.bacc as bacc
    from concourse.bass_utils import run_bass_kernel_spmd

    x = {k: np.asarray(v) for k, v in x.items()}

    def tiles(v):
        return v.reshape(-1, P, v.shape[-1]).transpose(1, 0, 2)

    def table(v):
        v = v.reshape(4, P, 1, XD // 2)
        return np.broadcast_to(v, (4, P, 4, XD // 2)).transpose(1, 0, 2, 3).reshape(P, 512)

    xf = x["x"].reshape(T, D)
    wq = x["L0_xattn_Wq"].reshape(D, HP, 2, 1, XD)
    wq = np.broadcast_to(wq, (D, HP, 2, 2, XD)).reshape(D, HP, 256)
    wkv = x["L0_xattn_Wkv"]
    wk = wkv[:, :XH * XD].reshape(D, HP, 2, 2, XD // 2).transpose(0, 1, 3, 2, 4)
    wkv = np.concatenate([wk.reshape(D, HP, P), wkv[:, XH * XD:].reshape(D, HP, P)], 2)
    qk = x["L0_ffn_Wqkv"][:, :2 * D].reshape(D, 2, NQ, 4, 1, FD)
    qk = np.broadcast_to(qk, (D, 2, NQ, 4, 4, FD)).reshape(D, 2 * NQ * P)
    bqk = x["L0_ffn_bqkv"][:2 * D].reshape(2 * NQ, 4, 1, FD)
    bqk = np.broadcast_to(bqk, (2 * NQ, 4, 4, FD)).reshape(2 * NQ, P).T
    fc1 = x["L0_ffn_fc1_w"].transpose(0, 2, 1)
    fc2 = x["L0_ffn_fc2_w"].reshape(E, D, FT, P).transpose(0, 3, 2, 1).reshape(E, P, FT * D)
    fb1 = x["L0_ffn_fc1_b"].reshape(E, FT, P).transpose(0, 2, 1)
    const, a_rope = constants()
    arrays = {
        "const": const,
        "a_rope": a_rope,
        "x_rope": np.stack([table(x["L0_xattn_cos"]), table(x["L0_xattn_sin"])], 1),
        "x_tok": tiles(xf),
        "xT": xf.T,
        "ctx_tok": tiles(x["ctx_1024"].reshape(B * SC, D)),
        "vec": np.concatenate([np.stack([x["L0_xattn_ln_ctx_g"], x["L0_xattn_ln_ctx_b"],
                                         x["L0_xattn_ln_lat_g"], x["L0_xattn_ln_lat_b"],
                                         x["L0_ffn_ln1_w"], x["L0_ffn_ln1_b"],
                                         x["L0_ffn_ln2_w"], x["L0_ffn_ln2_b"]], 1), bqk], 1),
        "rows": np.broadcast_to(np.stack([x["L0_xattn_bo"], x["L0_ffn_bo"],
                                          x["L0_ffn_bqkv"][2 * D:]])[None], (P, 3, D)),
        "a_w": np.concatenate([x["L0_attn_wq"], x["L0_attn_wk"], x["L0_attn_wv"]], 2),
        "a_wo": x["L0_attn_wo"].transpose(1, 0, 2),
        "x_w": np.concatenate([wq, wkv], 2),
        "x_wo": tiles(x["L0_xattn_Wo"]),
        "f_wqk": qk,
        "f_wvo": np.stack([x["L0_ffn_Wqkv"][:, 2 * D:], x["L0_ffn_Wo"]], 1),
        "gate_w": x["L0_ffn_gate_W"],
        "fc2_b": np.concatenate([x["L0_ffn_fc2_b"]] * 2, 0),
        "experts": np.concatenate([fc1, fc2, fb1], 2),
    }
    arrays = {k: np.ascontiguousarray(v) for k, v in arrays.items()}
    nc = bacc.Bacc("TRN2", target_bir_lowering=False, num_devices=1)
    a = {k: nc.dram_tensor("in_" + k, v.shape, mybir.dt.from_np(v.dtype), kind="ExternalInput").ap()
         for k, v in arrays.items()}
    out = nc.dram_tensor("out_dram", (P, NT, D), F32, kind="ExternalOutput").ap()
    build_program(nc, a, out)
    r = run_bass_kernel_spmd(nc, [{"in_" + k: v for k, v in arrays.items()}], core_ids=[0])
    return r.results[0]["out_dram"].transpose(1, 0, 2).reshape(B, S, D)
```
